# Optimizing a Trainium2 kernel written in Bass

```python
import numpy as np
import jax
import jax.numpy as jnp

def _softmax(x, axis=-1):
    return jax.nn.softmax(x, axis=axis)

def _gelu(x):
    return jax.nn.gelu(x, approximate=True)

def _silu(x):
    return jax.nn.silu(x)

def _sigmoid(x):
    return jax.nn.sigmoid(x)

def _layernorm(x, axis=-1, eps=1e-05):
    m = jnp.mean(x, axis=axis, keepdims=True)
    v = jnp.var(x, axis=axis, keepdims=True)
    return (x - m) / jnp.sqrt(v + eps)

def _scatter_add(tgt, idx, src, axis=0):
    return tgt.at[idx].add(src)

def _segment_sum(src, seg, n):
    return jax.ops.segment_sum(src, seg, n)
kernel_name = 'mk_decoder_preln_d1_seqx_r4_1c1488'

def setup_inputs(seed: int=0):
    np.random.seed(seed)
    _w = jnp.asarray

    def _rec_inputs():
        import jax
        import jax.numpy as jnp
        _rk = jax.random.key(seed)
        x = -0.0002928 + 1 * jax.random.normal(jax.random.fold_in(_rk, 1), (8, 512, 256), jnp.float32)
        _lenS = 512 - jax.random.randint(jax.random.fold_in(_rk, 7), (8,), 0, max(1, 512 // 4) + 1, jnp.int32)
        _lenS2 = 512 - jax.random.randint(jax.random.fold_in(_rk, 8), (8,), 0, max(1, 512 // 4) + 1, jnp.int32)
        _ctx_1024P = jax.random.normal(jax.random.fold_in(_rk, 11), (8, 16, 256), jnp.float32)
        _ctx_1024c = jax.random.dirichlet(jax.random.fold_in(_rk, 511), 0.3 * jnp.ones((16,), jnp.float32), (8, 512))
        _ctx_1024t = jnp.einsum('bsk,bkd->bsd', _ctx_1024c, _ctx_1024P)
        _ctx_1024t = _ctx_1024t * jax.lax.rsqrt(jnp.mean(jnp.square(_ctx_1024t)) + 1e-12) * 0.953939
        ctx_1024 = -1.78809e-06 + 0.0312453 * (_ctx_1024t + 0.3 * jax.random.normal(jax.random.fold_in(_rk, 611), (8, 512, 256), jnp.float32))
        return (x, ctx_1024)
    x, ctx_1024 = _rec_inputs()

    def _L0_attn_setup():
        import jax, jax.numpy as jnp
        import numpy as np
        EPS = 1e-05
        NUM_HEADS = 16
        FEATURE_DIM = 16
        CHUNK = 64

        def _phi(x):
            f = x.shape[-1]
            return (x[..., :, None] * x[..., None, :]).reshape(*x.shape[:-1], f * f)
        key = jax.random.key(seed)
        ks = jax.random.split(key, 5)
        b, l, d = (4, 512, 256)
        h, f = (NUM_HEADS, FEATURE_DIM)
        hd = d // h
        scale = 0.02
        return {'hidden_states': jax.random.normal(ks[0], (b, l, d), jnp.float32), 'Wq': jax.random.normal(ks[1], (d, h * f), jnp.float32) * scale, 'Wk': jax.random.normal(ks[2], (d, h * f), jnp.float32) * scale, 'Wv': jax.random.normal(ks[3], (d, h * hd), jnp.float32) * scale, 'Wo': jax.random.normal(ks[4], (h * hd, d), jnp.float32) * scale}
    _L0_attn_all = _L0_attn_setup()
    _L0_attn_in = {k: v for k, v in _L0_attn_all.items() if k in ('Wq', 'Wk', 'Wv', 'Wo')}
    del _L0_attn_all

    def _L0_xattn_setup():
        import jax, jax.numpy as jnp
        import numpy as np
        E, TPE, H, F = (64, 64, 256, 256)
        key = jax.random.key(seed)
        k1, k2, k3, k4 = jax.random.split(key, 4)
        scale = 1.0 / np.sqrt(H)
        return {'x': jax.random.normal(k1, (E, TPE, H), dtype=jnp.float32), 'w1': jax.random.normal(k2, (E, F, H), dtype=jnp.float32) * scale, 'v1': jax.random.normal(k3, (E, F, H), dtype=jnp.float32) * scale, 'w2': jax.random.normal(k4, (E, F, H), dtype=jnp.float32) * scale}
    _L0_xattn_all = _L0_xattn_setup()
    _L0_xattn_in = {k: v for k, v in _L0_xattn_all.items() if k in ()}
    del _L0_xattn_all

    def _L0_ffn_setup():
        import jax, jax.numpy as jnp
        import numpy as np
        B, S, D_MODEL, D_HIDDEN = (4, 512, 256, 1024)

        def act_quant(x):
            scale = 127.0 / jnp.clip(jnp.max(jnp.abs(x), axis=-1, keepdims=True), 1e-05)
            return jnp.clip(jnp.round(x * scale), -128, 127) / scale

        def weight_quant(w):
            scale = 1.0 / jnp.clip(jnp.mean(jnp.abs(w)), 1e-05)
            return jnp.clip(jnp.round(w * scale), -1, 1) / scale

        def bit_linear(x, w):
            xq = x + jax.lax.stop_gradient(act_quant(x) - x)
            wq = w + jax.lax.stop_gradient(weight_quant(w) - w)
            return jnp.einsum('bsd,hd->bsh', xq, wq)

        def depthwise_conv1d(x_bcl, w, b):
            y = jax.lax.conv_general_dilated(x_bcl, w, window_strides=(1,), padding=[(1, 1)], dimension_numbers=('NCH', 'OIH', 'NCH'), feature_group_count=x_bcl.shape[1])
            return y + b[None, :, None]
        key = jax.random.key(seed)
        ks = jax.random.split(key, 5)
        lim1 = 1.0 / np.sqrt(D_MODEL)
        lim2 = 1.0 / np.sqrt(D_HIDDEN)
        limc = 1.0 / np.sqrt(3.0)
        return {'x': jax.random.normal(ks[0], (B, S, D_MODEL), dtype=jnp.float32), 'w1': jax.random.uniform(ks[1], (D_HIDDEN, D_MODEL), jnp.float32, -lim1, lim1), 'conv_w': jax.random.uniform(ks[2], (D_HIDDEN, 1, 3), jnp.float32, -limc, limc), 'conv_b': jax.random.uniform(ks[3], (D_HIDDEN,), jnp.float32, -limc, limc), 'w2': jax.random.uniform(ks[4], (D_MODEL, D_HIDDEN), jnp.float32, -lim2, lim2)}
    _L0_ffn_all = _L0_ffn_setup()
    _L0_ffn_in = {k: v for k, v in _L0_ffn_all.items() if k in ('w1', 'conv_w', 'conv_b', 'w2')}
    del _L0_ffn_all
    return {'x': x, 'ctx_1024': ctx_1024, 'L0_attn_Wq': _L0_attn_in['Wq'], 'L0_attn_Wk': _L0_attn_in['Wk'], 'L0_attn_Wv': _L0_attn_in['Wv'], 'L0_attn_Wo': _L0_attn_in['Wo'], 'L0_ffn_w1': _L0_ffn_in['w1'], 'L0_ffn_conv_w': _L0_ffn_in['conv_w'], 'L0_ffn_conv_b': _L0_ffn_in['conv_b'], 'L0_ffn_w2': _L0_ffn_in['w2']}

def reference(x, ctx_1024, L0_attn_Wq, L0_attn_Wk, L0_attn_Wv, L0_attn_Wo, L0_ffn_w1, L0_ffn_conv_w, L0_ffn_conv_b, L0_ffn_w2):
    import jax
    import jax.numpy as jnp

    def _L0_attn_ref(hidden_states, Wq, Wk, Wv, Wo):
        import jax, jax.numpy as jnp
        import numpy as np
        EPS = 1e-05
        NUM_HEADS = 16
        FEATURE_DIM = 16
        CHUNK = 64

        def _phi(x):
            f = x.shape[-1]
            return (x[..., :, None] * x[..., None, :]).reshape(*x.shape[:-1], f * f)
        b, l, d = hidden_states.shape
        h, f = (NUM_HEADS, FEATURE_DIM)
        hd = d // h
        q = (hidden_states @ Wq).reshape(b, l, h, f).transpose(0, 2, 1, 3)
        k = (hidden_states @ Wk).reshape(b, l, h, f).transpose(0, 2, 1, 3)
        v = (hidden_states @ Wv).reshape(b, l, h, hd).transpose(0, 2, 1, 3)
        q = q * f ** (-0.5)
        n = l // CHUNK
        qc = q.reshape(b, h, n, CHUNK, f)
        kc = k.reshape(b, h, n, CHUNK, f)
        vc = v.reshape(b, h, n, CHUNK, hd)
        phi_q = _phi(qc)
        phi_k = _phi(kc)
        mask = jnp.tril(jnp.ones((CHUNK, CHUNK), dtype=q.dtype))

        def step(carry, inp):
            S, z = carry
            pq, pk, qi, ki, vi = inp
            inter_o = jnp.einsum('bhcf,bhfd->bhcd', pq, S)
            inter_z = jnp.einsum('bhcf,bhf->bhc', pq, z)
            A = jnp.einsum('bhcf,bhsf->bhcs', qi, ki) ** 2 * mask
            intra_o = jnp.einsum('bhcs,bhsd->bhcd', A, vi)
            intra_z = A.sum(-1)
            o = (inter_o + intra_o) / (inter_z + intra_z + EPS)[..., None]
            S = S + jnp.einsum('bhcf,bhcd->bhfd', pk, vi)
            z = z + pk.sum(2)
            return ((S, z), o)
        f2 = f * f
        S0 = jnp.zeros((b, h, f2, hd), q.dtype)
        z0 = jnp.zeros((b, h, f2), q.dtype)
        xs = (jnp.moveaxis(phi_q, 2, 0), jnp.moveaxis(phi_k, 2, 0), jnp.moveaxis(qc, 2, 0), jnp.moveaxis(kc, 2, 0), jnp.moveaxis(vc, 2, 0))
        _, o = jax.lax.scan(step, (S0, z0), xs)
        o = jnp.moveaxis(o, 0, 2).reshape(b, h, l, hd)
        o = o.transpose(0, 2, 1, 3).reshape(b, l, h * hd)
        return o @ Wo

    def _L0_xattn_ref(x, w1, v1, w2):
        import jax, jax.numpy as jnp
        import numpy as np
        E, TPE, H, F = (64, 64, 256, 256)
        h1 = jnp.einsum('eth,efh->etf', x, w1)
        h2 = jnp.einsum('eth,efh->etf', x, v1)
        g = jax.nn.gelu(h1, approximate=False) * h2
        return jnp.einsum('etf,efh->eth', g, w2)

    def _L0_ffn_ref(x, w1, conv_w, conv_b, w2):
        import jax, jax.numpy as jnp
        import numpy as np
        B, S, D_MODEL, D_HIDDEN = (4, 512, 256, 1024)

        def act_quant(x):
            scale = 127.0 / jnp.clip(jnp.max(jnp.abs(x), axis=-1, keepdims=True), 1e-05)
            return jnp.clip(jnp.round(x * scale), -128, 127) / scale

        def weight_quant(w):
            scale = 1.0 / jnp.clip(jnp.mean(jnp.abs(w)), 1e-05)
            return jnp.clip(jnp.round(w * scale), -1, 1) / scale

        def bit_linear(x, w):
            xq = x + jax.lax.stop_gradient(act_quant(x) - x)
            wq = w + jax.lax.stop_gradient(weight_quant(w) - w)
            return jnp.einsum('bsd,hd->bsh', xq, wq)

        def depthwise_conv1d(x_bcl, w, b):
            y = jax.lax.conv_general_dilated(x_bcl, w, window_strides=(1,), padding=[(1, 1)], dimension_numbers=('NCH', 'OIH', 'NCH'), feature_group_count=x_bcl.shape[1])
            return y + b[None, :, None]
        h = bit_linear(x, w1)
        h = depthwise_conv1d(h.transpose(0, 2, 1), conv_w, conv_b)
        h = h.transpose(0, 2, 1)
        h = jax.nn.silu(h)
        return bit_linear(h, w2)
    x = x + _L0_attn_ref(_layernorm(x, axis=-1), L0_attn_Wq, L0_attn_Wk, L0_attn_Wv, L0_attn_Wo)
    x = x + _L0_xattn_ref(_layernorm(x, axis=-1), ctx_1024, ctx_1024, ctx_1024)
    x = x + _L0_ffn_ref(_layernorm(x, axis=-1), L0_ffn_w1, L0_ffn_conv_w, L0_ffn_conv_b, L0_ffn_w2)
    return x

_drawn_inputs = setup_inputs


def setup_inputs(seed=0):
    import zlib

    import numpy as np

    out = dict(_drawn_inputs(seed))
    spreads = {}
    factors = {'L0_attn_Wq': 4.605, 'L0_attn_Wk': 4.44, 'L0_attn_Wv': 3.476, 'L0_attn_Wo': 3.28}
    for name, (base, spread) in spreads.items():
        noise = np.random.default_rng([zlib.crc32(name.encode()), seed]).standard_normal(out[name].shape)
        drawn = base * np.exp(spread * noise) if base else spread * noise
        out[name] = jnp.asarray(drawn.astype(out[name].dtype))
    for name, factor in factors.items():
        out[name] = (out[name] * factor).astype(out[name].dtype)
    return out
```

```python
import concourse.bass as bass
from concourse import mybir
from contextlib import ExitStack


def decoder_layer(nc, x, ctx_rows, ctx_cols, w_qk, w_v, w_o, w_up, conv_w, conv_b, w_down, out):
    fp32 = mybir.dt.float32
    bf16 = mybir.dt.bfloat16
    ALU = mybir.AluOpType
    ACT = mybir.ActivationFunctionType
    AX = mybir.AxisListType

    B, L, D = x.shape
    F = w_up.shape[1]
    P = 128
    T = L // P
    KD = D // P
    NF = F // P
    HEADS, HD = 16, 16
    GROUP = 4
    GROUPS = HEADS // GROUP
    HALF = HEADS // 2
    BANK = 512
    QSCALE = float(HD) ** -0.5
    LN_EPS = 1e-5
    DEN_EPS = 1e-5
    CLIP = 1e-5
    MAGIC = 12582912.0
    PIECES = GROUP + 1
    NP = GROUPS * PIECES
    TILE_AT = [0, 640, None, 512]
    TILE2_AT = GROUP * 1024

    Q_PART = [0, 0, 1, 1, 0, 2, 1, 2]
    K_PART = [0, 1, 0, 1, 2, 0, 2, 1]
    NG = len(Q_PART)

    with ExitStack() as stack:
        def sb(name, shape, dt=fp32):
            return stack.enter_context(nc.sbuf_tensor(name, shape, dt))

        def sem(name):
            return stack.enter_context(nc.semaphore(name))

        ident = sb("ident", [P, P])
        identb = sb("identb", [P, P], bf16)
        ones = sb("ones", [P, P])
        neg_half = sb("neg_half", [P, T])
        wqk = sb("wqk", [P, KD, 2 * D])
        wv = sb("wv", [P, KD, D])
        wo = sb("wo", [P, KD, D])
        w_up_q = sb("w_up_q", [P, KD, F], bf16)
        w_dn_q = sb("w_dn_q", [P, NF, D], bf16)
        cw = sb("cw", [P, NF, 3])
        cb = sb("cb", [P, NF])
        wsum = sb("wsum", [P, 2])
        wmean = sb("wmean", [P, 2])
        wscale = sb("wscale", [P, 2])

        x_in = sb("x_in", [P, T, D])
        tok = sb("tok", [P, T, D])
        norm1T = sb("norm1T", [P, KD, L])
        parts = [sb(f"part_{n}", [P, 4, L], bf16) for n in ("high", "mid", "low")]
        rest = sb("rest", [P, 2, L])
        Qs = sb("Qs", [P, HALF, 2, L], bf16)
        Ks = sb("Ks", [P, HALF, 2, L], bf16)
        V1 = sb("V1", [P, T, HEADS, 32])
        st1, mv1, ve1, rs1 = sb("st1", [P, T, 6]), sb("mv1", [P, T, 2]), sb("ve1", [P, T]), sb("rs1", [P, T])

        x_res = sb("x_res", [P, T, D])
        A = sb("A", [P, 2, GROUP * 1280])
        oT = sb("oT", [P, GROUPS, L])
        gT = oT
        den = sb("den", [P, T, HEADS])
        rden = sb("rden", [P, T, HEADS])
        rowT = sb("rowT", [P, KD, L])
        x1 = sb("x1", [P, T, D])
        x2 = sb("x2", [P, T, D])
        ctxT = sb("ctxT", [P, KD, L])
        ctxR = sb("ctxR", [P, T, D])
        gl = sb("gl", [P, 2, L])
        st2, mv2, ve2, rs2 = sb("st2", [P, T, 6]), sb("mv2", [P, T, 2]), sb("ve2", [P, T]), sb("rs2", [P, T])

        xn3 = sb("xn3", [P, T, D])
        xq = sb("xq", [P, T, D], bf16)
        xqT = sb("xqT", [P, KD, L], bf16)
        sB = sb("sB", [P, L])
        hs = sb("hs", [P, 2, L + 2])
        cv = sb("cv", [P, 2, L])
        act_out = sb("act_out", [P, NF, L])
        w_raw = act_out[:, :, :].rearrange("p f t -> p (f t)")
        am = sb("am", [P, L])
        s2B = sB
        hq = sb("hq", [P, NF, L], bf16)
        st3, mv3, ve3, rs3 = sb("st3", [P, T, 6]), sb("mv3", [P, T, 2]), sb("ve3", [P, T]), sb("rs3", [P, T])
        mx3, sc3, sdq = sb("mx3", [P, T]), sb("sc3", [P, T]), sb("sdq", [P, T])
        mx4, sc4, sdq4 = sb("mx4", [P, T]), sb("sc4", [P, T]), sb("sdq4", [P, T])

        M = stack.enter_context(nc.psum_tensor("M", [P, 6, BANK], fp32))
        FB = stack.enter_context(nc.psum_tensor("FB", [P, 2, BANK], fp32))

        per = {}

        def psem(name, n):
            per[name] = n
            return sem(name)

        w_qkv_loaded = sem("w_qkv_loaded")
        w_rest_loaded = sem("w_rest_loaded")
        waited = sem("waited")
        raw_loaded = sem("raw_loaded")
        consts_ready = sem("consts_ready")
        setup_dve = sem("setup_dve")
        wsum_ready = sem("wsum_ready")
        wtotal_ready = sem("wtotal_ready")
        weights_quantised = sem("weights_quantised")

        x_in_loaded = psem("x_in_loaded", 16)
        var1_ready = psem("var1_ready", 1)
        rstd1_ready = psem("rstd1_ready", 1)
        xn1_ready = psem("xn1_ready", 1)
        xn1T_in_psum = psem("xn1T_in_psum", KD)
        xn1T_ready = psem("xn1T_ready", KD)
        qk_in_psum = psem("qk_in_psum", 4)
        high_ready = psem("high_ready", 4)
        rest_ready = psem("rest_ready", 4)
        mid_ready = psem("mid_ready", 2)
        low_ready = psem("low_ready", 2)
        spread = psem("spread", 2 * NG * 16)
        v_in_psum = psem("v_in_psum", 2)
        v_ready = psem("v_ready", 2)
        pre_chain = psem("pre_chain", 2)

        x_res_ready = psem("x_res_ready", 16)
        ctx_loaded = psem("ctx_loaded", 32)
        scores_ready = psem("scores_ready", NP)
        squared = psem("squared", NP)
        masked = psem("masked", 3 * GROUPS)
        values_summed = psem("values_summed", GROUPS)
        oT_ready = psem("oT_ready", GROUPS)
        o_in_psum = psem("o_in_psum", T)
        o_normed = psem("o_normed", 1)
        onT_in_psum = psem("onT_in_psum", KD)
        onT_ready = psem("onT_ready", KD)
        wo_in_psum = psem("wo_in_psum", 2)
        x1_ready = psem("x1_ready", 2)
        var2_ready = psem("var2_ready", 1)
        rstd2_ready = psem("rstd2_ready", 1)
        xn2_ready = psem("xn2_ready", 1)
        xn2T_in_psum = psem("xn2T_in_psum", KD)
        xn2T_ready = psem("xn2T_ready", KD)
        h1_in_psum = psem("h1_in_psum", T)
        gelu_ready = psem("gelu_ready", T)
        gated = psem("gated", T)
        mix_in_psum = psem("mix_in_psum", 2)
        x2_ready = psem("x2_ready", 2)
        main_chain = psem("main_chain", 4)

        var3_ready = psem("var3_ready", 1)
        rstd3_ready = psem("rstd3_ready", 1)
        xq_ready = psem("xq_ready", 1)
        xqT_in_psum = psem("xqT_in_psum", 1)
        xqT_ready = psem("xqT_ready", 1)
        s_in_psum = psem("s_in_psum", 1)
        sB_ready = psem("sB_ready", 1)
        up_in_psum = psem("up_in_psum", NF)
        hs_ready = psem("hs_ready", NF)
        centre_ready = psem("centre_ready", NF)
        conv_ready = psem("conv_ready", NF)
        silu_ready = psem("silu_ready", NF)
        am_ready = psem("am_ready", 1)
        amT_in_psum = psem("amT_in_psum", 1)
        s2_ready = psem("s2_ready", 1)
        s2_in_psum = psem("s2_in_psum", 1)
        s2B_ready = psem("s2B_ready", 1)
        scaled = psem("scaled", NF)
        hq_ready = psem("hq_ready", NF // 2)
        down_in_psum = psem("down_in_psum", 2)
        out_ready = psem("out_ready", 1)
        rows_free = psem("rows_free", 16)
        ffn_chain = psem("ffn_chain", 10 + NF)
        hidden_chain = psem("hidden_chain", 5)

        def count(s, b, n):
            return per[s.name] * b + n

        def due(value):
            return not isinstance(value, int) or value > 0

        def settle(eng):
            eng.sem_inc(waited, 1)

        class Chain:

            def __init__(self, eng, sem, b):
                self.eng, self.sem, self.b, self.n = eng, sem, b, 0

            def link(self, ins):
                self.n += 1
                ins.then_inc(self.sem, 1)
                self.eng.wait_ge(self.sem, count(self.sem, self.b, self.n))

            def end(self):
                assert self.n == per[self.sem.name], (self.sem.name, self.n)

        def rows(dram, b):
            return dram[bass.ds(b, 1), :, :].rearrange("o (t p) d -> p (o t) d", p=P)

        block = stack.enter_context(nc.Block())

        @block.sync
        def _(sp):
            def load_x(b):
                if due(c := count(xn1_ready, b, 0)):
                    sp.wait_ge(xn1_ready, c)
                settle(sp)
                if due(c := count(x_res_ready, b, 0)):
                    sp.wait_ge(x_res_ready, c)
                settle(sp)
                sp.dma_start(x_in[:, :, :], rows(x, b)).then_inc(x_in_loaded, 16)

            def copy_x(b):
                sp.wait_ge(x_in_loaded, count(x_in_loaded, b, 16))
                if due(c := count(x1_ready, b, 0)):
                    sp.wait_ge(x1_ready, c)
                sp.dma_start(x_res[:, :, :], x_in[:, :, :]).then_inc(x_res_ready, 16)

            def load_ctx(b):
                if due(c := count(mix_in_psum, b, 0)):
                    sp.wait_ge(mix_in_psum, c)
                settle(sp)
                sp.dma_start(ctxT[:, :, :], ctx_cols[bass.ds(b, 1), :, :].rearrange(
                    "o (k p) t -> p (o k) t", p=P)).then_inc(ctx_loaded, 16)
                sp.dma_start(ctxR[:, :, :], rows(ctx_rows, b)).then_inc(ctx_loaded, 16)

            def spread_side(b, side):
                dst, which = ((Qs, Q_PART), (Ks, K_PART))[side]
                if due(c := count(scores_ready, b, 0)):
                    sp.wait_ge(scores_ready, c)
                settle(sp)
                for part, ready, n in ((0, high_ready, 2), (1, mid_ready, 1), (2, low_ready, 1)):
                    sp.wait_ge(ready, count(ready, b, n * (side + 1)))
                    for g in range(NG):
                        if which[g] == part:
                            sp.dma_start(dst[16 * g:16 * g + 16, :, :, :].rearrange("d h m t -> d (h m t)"),
                                         parts[part][:, 2 * side:2 * side + 2, :].rearrange("p m t -> p (m t)")
                                         ).then_inc(spread, 16)

            def store(b):
                sp.wait_ge(out_ready, count(out_ready, b, 1))
                settle(sp)
                sp.dma_start(rows(out, b), xn3[:, :, :]).then_inc(rows_free, 16)

            def iteration(b, ahead, behind):
                if ahead:
                    load_x(b + 1)
                load_ctx(b)
                if ahead:
                    spread_side(b + 1, 0)
                    copy_x(b + 1)
                    spread_side(b + 1, 1)
                if behind:
                    store(b - 1)

            sp.sem_inc(rows_free, 16)
            load_x(0)
            sp.dma_start(wqk[:, :, :], w_qk.rearrange("(k p) n -> p k n", p=P)).then_inc(w_qkv_loaded, 16)
            sp.dma_start(wv[:, :, :], w_v.rearrange("(k p) n -> p k n", p=P)).then_inc(w_qkv_loaded, 16)
            copy_x(0)
            spread_side(0, 0)
            sp.dma_start(wo[:, :, :], w_o.rearrange("(k p) n -> p k n", p=P)).then_inc(w_rest_loaded, 16)
            spread_side(0, 1)
            sp.dma_start(cw[:, :, :], conv_w).then_inc(w_rest_loaded, 16)
            sp.dma_start(cb[:, :], conv_b).then_inc(w_rest_loaded, 16)
            sp.dma_start(w_raw[:, 0:KD * F].rearrange("p (k n) -> p k n", k=KD),
                         w_up.rearrange("(k p) n -> p k n", p=P)).then_inc(raw_loaded, 16)
            sp.dma_start(w_raw[:, KD * F:2 * KD * F].rearrange("p (f n) -> p f n", f=NF),
                         w_down.rearrange("(f p) n -> p f n", p=P)).then_inc(raw_loaded, 16)
            iteration(0, True, False)
            with sp.Fori(1, B - 1) as b:
                iteration(b, True, True)
            iteration(B - 1, False, True)
            store(B - 1)
            sp.wait_ge(rows_free, 16 * B + 16)

        @block.gpsimd
        def _(pool):
            def rstd(b, var_ready, ve, rs, ready):
                pool.wait_ge(var_ready, count(var_ready, b, 1))
                pool.tensor_tensor(rs[:, :], ve[:, :], neg_half[:, :], ALU.pow).then_inc(ready, 1)

            def mask(b, g):
                a = A[:, g % 2, :]
                pool.wait_ge(squared, count(squared, b, PIECES * g + GROUP))
                settle(pool)
                first = a[:, 0:TILE2_AT].rearrange("p (h n) -> p h n", h=GROUP)[:, :, 0:P]
                pool.affine_select(out=first, in_=first, compare_op=ALU.is_ge, fill=0.0, base=0,
                                   pattern=[[0, GROUP], [1, P]], channel_multiplier=-1).then_inc(masked, 1)
                pair = a[:, 0:TILE2_AT].rearrange("p (h n) -> p h n", h=GROUP)[:, :, TILE_AT[3]:TILE_AT[3] + 2 * P]\
                    .rearrange("p h (j c) -> p h j c", j=2)
                pool.affine_select(out=pair, in_=pair, compare_op=ALU.is_ge, fill=0.0, base=0,
                                   pattern=[[0, GROUP], [0, 2], [1, P]], channel_multiplier=-1).then_inc(masked, 1)
                pool.wait_ge(squared, count(squared, b, PIECES * g + PIECES))
                settle(pool)
                second = a[:, TILE2_AT:TILE2_AT + 1024].rearrange("p (h n) -> p h n", h=GROUP)[:, :, 0:P]
                pool.affine_select(out=second, in_=second, compare_op=ALU.is_ge, fill=0.0, base=0,
                                   pattern=[[0, GROUP], [1, P]], channel_multiplier=-1).then_inc(masked, 1)

            def low_part(b, side):
                pool.wait_ge(rest_ready, count(rest_ready, b, 2 * side + 2))
                pool.wait_ge(mid_ready, count(mid_ready, b, side + 1))
                pool.tensor_tensor(parts[2][:, 2 * side:2 * side + 2, :], rest[:, :, :],
                                   parts[1][:, 2 * side:2 * side + 2, :], ALU.subtract).then_inc(low_ready, 1)

            def scale_hidden(b, f0, f1):
                pool.wait_ge(s2B_ready, count(s2B_ready, b, 1))
                for f in range(f0, f1):
                    pool.tensor_tensor(act_out[:, f, :], act_out[:, f, :], s2B[:, :], ALU.mult)\
                        .then_inc(scaled, 1)

            def iteration(b, ahead, behind):
                if behind:
                    rstd(b - 1, var3_ready, ve3, rs3, rstd3_ready)
                if ahead:
                    rstd(b + 1, var1_ready, ve1, rs1, rstd1_ready)
                for g in range(GROUPS):
                    mask(b, g)
                if ahead:
                    low_part(b + 1, 0)
                rstd(b, var2_ready, ve2, rs2, rstd2_ready)
                if ahead:
                    low_part(b + 1, 1)
                if behind:
                    scale_hidden(b - 1, 0, NF)

            pool.memset(ident[:, :], 0.0).then_inc(consts_ready, 1)
            pool.memset(ones[:, :], 1.0).then_inc(consts_ready, 1)
            pool.memset(neg_half[:, :], -0.5).then_inc(consts_ready, 1)
            pool.wait_ge(consts_ready, 3)
            pool.affine_select(out=ident[:, :], in_=ident[:, :], compare_op=ALU.not_equal, fill=1.0,
                               base=0, pattern=[[-1, P]], channel_multiplier=1).then_inc(consts_ready, 1)
            pool.memset(V1[:, :, :, HD:32], 0.0).then_inc(consts_ready, 1)
            pool.wait_ge(consts_ready, 5)
            pool.memset(V1[:, :, :, HD:HD + 1], 1.0).then_inc(consts_ready, 1)
            pool.memset(hs[:, :, 0:1], 0.0).then_inc(consts_ready, 1)
            pool.memset(hs[:, :, L + 1:L + 2], 0.0).then_inc(consts_ready, 1)
            rstd(0, var1_ready, ve1, rs1, rstd1_ready)
            low_part(0, 0)
            low_part(0, 1)
            iteration(0, True, False)
            with pool.Fori(1, B - 1) as b:
                iteration(b, True, True)
            iteration(B - 1, False, True)
            rstd(B - 1, var3_ready, ve3, rs3, rstd3_ready)
            scale_hidden(B - 1, 0, NF)

        @block.scalar
        def _(act):
            def xn1T_copy(b):
                for k in range(KD):
                    act.wait_ge(xn1T_in_psum, count(xn1T_in_psum, b, k + 1))
                    act.activation(norm1T[:, k, :], M[:, 4 + k, :], ACT.Copy).then_inc(xn1T_ready, 1)

            def high_part(b, m):
                act.wait_ge(qk_in_psum, count(qk_in_psum, b, m + 1))
                if m % 2 == 0:
                    if due(c := count(spread, b, 0)):
                        act.wait_ge(spread, c)
                act.activation(parts[0][:, m, :], M[:, 4 + m % 2, :], ACT.Copy).then_inc(high_ready, 1)

            def v_copy(b):
                for j in range(2):
                    act.wait_ge(v_in_psum, count(v_in_psum, b, j + 1))
                    act.activation(V1[:, 2 * j:2 * j + 2, :, 0:HD],
                                   M[:, j, :].rearrange("p (t h d) -> p t h d", t=2, h=HEADS),
                                   ACT.Copy).then_inc(v_ready, 1)

            def square(b, g, n):
                p = PIECES * g + n
                act.wait_ge(scores_ready, count(scores_ready, b, p + 1))
                if n == 0:
                    if due(c := count(values_summed, b, g - 1)):
                        act.wait_ge(values_summed, c)
                act.activation(A[:, g % 2, n * 1024:(n + 1) * 1024],
                               M[:, 2 * (p % 2):2 * (p % 2) + 2, :].rearrange("p a n -> p (a n)"),
                               ACT.Square, scale=QSCALE).then_inc(squared, 1)

            def oT_copy(b, g):
                act.wait_ge(values_summed, count(values_summed, b, g + 1))
                if g == 0:
                    if due(c := count(mix_in_psum, b, 0)):
                        act.wait_ge(mix_in_psum, c)
                act.activation(oT[:, g, :], M[:, 4 + g % 2, :], ACT.Copy).then_inc(oT_ready, 1)

            def rowT_copy(b, in_psum, bank, ready):
                for k in range(KD):
                    act.wait_ge(in_psum, count(in_psum, b, k + 1))
                    act.activation(rowT[:, k, :], M[:, bank + k, :], ACT.Copy).then_inc(ready, 1)

            def gelu(b):
                for f in range(T):
                    act.wait_ge(h1_in_psum, count(h1_in_psum, b, f + 1))
                    if due(c := count(gated, b, f - 1)):
                        act.wait_ge(gated, c)
                    act.activation(gl[:, f % 2, :], M[:, (0, 1, 4, 5)[f], :], ACT.Gelu).then_inc(gelu_ready, 1)

            def xqT_copy(b):
                act.wait_ge(xqT_in_psum, count(xqT_in_psum, b, 1))
                act.activation(xqT[:, :, :].rearrange("p k t -> p (k t)"), FB[:, 0, :].bitcast(bf16), ACT.Copy).then_inc(xqT_ready, 1)
                act.wait_ge(s_in_psum, count(s_in_psum, b, 1))
                act.activation(sB[:, :], FB[:, 1, :], ACT.Copy).then_inc(sB_ready, 1)

            def centre_tap(b, f):
                act.wait_ge(hs_ready, count(hs_ready, b, f + 1))
                if f >= 2:
                    if due(c := count(silu_ready, b, f - 1)):
                        act.wait_ge(silu_ready, c)
                act.activation(cv[:, f % 2, :], hs[:, f % 2, 1:L + 1], ACT.Identity,
                               scale=cw[:, f, 1:2], bias=cb[:, f:f + 1]).then_inc(centre_ready, 1)

            def silu(b, f):
                act.wait_ge(conv_ready, count(conv_ready, b, f + 1))
                act.activation(act_out[:, f, :], cv[:, f % 2, :], ACT.Silu).then_inc(silu_ready, 1)

            def s2B_copy(b):
                act.wait_ge(s2_in_psum, count(s2_in_psum, b, 1))
                act.activation(s2B[:, :], FB[:, 1, :], ACT.Copy).then_inc(s2B_ready, 1)

            def squares(b, g, n0=0, n1=PIECES):
                for n in range(n0, n1):
                    square(b, g, n)

            def attention(b, behind):
                squares(b, 0)
                squares(b, 1)
                if behind:
                    xqT_copy(b - 1)
                squares(b, 2, 0, 1)
                if behind:
                    centre_tap(b - 1, 0)
                squares(b, 2, 1, 2)
                if behind:
                    centre_tap(b - 1, 1)
                    silu(b - 1, 0)
                squares(b, 2, 2, 4)
                oT_copy(b, 0)
                squares(b, 2, 4)
                if behind:
                    centre_tap(b - 1, 2)
                    silu(b - 1, 1)
                squares(b, 3, 0, 1)
                if behind:
                    centre_tap(b - 1, 3)
                    silu(b - 1, 2)
                squares(b, 3, 1, 2)
                if behind:
                    centre_tap(b - 1, 4)
                    silu(b - 1, 3)
                squares(b, 3, 2, 3)
                oT_copy(b, 1)
                squares(b, 3, 3)
                if behind:
                    centre_tap(b - 1, 5)
                    silu(b - 1, 4)
                oT_copy(b, 2)
                if behind:
                    centre_tap(b - 1, 6)
                    silu(b - 1, 5)
                oT_copy(b, 3)
                if behind:
                    centre_tap(b - 1, 7)
                    silu(b - 1, 6)
                    silu(b - 1, 7)

            def iteration(b, ahead, behind):
                attention(b, behind)
                if ahead:
                    xn1T_copy(b + 1)
                    high_part(b + 1, 0)
                    high_part(b + 1, 1)
                rowT_copy(b, onT_in_psum, 0, onT_ready)
                if behind:
                    s2B_copy(b - 1)
                if ahead:
                    high_part(b + 1, 2)
                    high_part(b + 1, 3)
                    v_copy(b + 1)
                rowT_copy(b, xn2T_in_psum, 2, xn2T_ready)
                gelu(b)

            xn1T_copy(0)
            for m in range(4):
                high_part(0, m)
            v_copy(0)
            iteration(0, True, False)
            with act.Fori(1, B - 1) as b:
                iteration(b, True, True)
            iteration(B - 1, False, True)
            xqT_copy(B - 1)
            for f in range(NF):
                centre_tap(B - 1, f)
                if f >= 1:
                    silu(B - 1, f - 1)
            silu(B - 1, NF - 1)
            s2B_copy(B - 1)

        @block.vector
        def _(dve):
            def norm_stats(chain, src, st, mv, ve, var_ready):
                for t in range(T):
                    ins = dve.bn_stats(st[:, t, :], src[:, t, :])
                chain.link(ins)
                settle(dve)
                for t in range(T):
                    ins = dve.bn_aggr(mv[:, t, :], st[:, t, :])
                chain.link(ins)
                dve.tensor_scalar(ve[:, :], mv[:, :, 1], LN_EPS, None, ALU.add).then_inc(var_ready, 1)

            def norm_apply(dst, src, mv, rs):
                for t in range(T):
                    ins = dve.tensor_scalar(dst[:, t, :], src[:, t, :], mv[:, t, 0:1], rs[:, t:t + 1],
                                            ALU.subtract, ALU.mult)
                return ins

            def pre_stats(b):
                dve.wait_ge(x_in_loaded, count(x_in_loaded, b, 16))
                chain = Chain(dve, pre_chain, b)
                norm_stats(chain, x_in, st1, mv1, ve1, var1_ready)
                chain.end()

            def pre_norm(b):
                dve.wait_ge(rstd1_ready, count(rstd1_ready, b, 1))
                if due(c := count(xn2T_in_psum, b, -KD)):
                    dve.wait_ge(xn2T_in_psum, c)
                norm_apply(tok, x_in, mv1, rs1).then_inc(xn1_ready, 1)

            def split(b, side):
                for j in range(2):
                    m = 2 * side + j
                    dve.wait_ge(high_ready, count(high_ready, b, m + 1))
                    if due(c := count(low_ready, b, side)):
                        dve.wait_ge(low_ready, c)
                    dve.tensor_tensor(rest[:, j, :], M[:, 4 + j, :], parts[0][:, m, :], ALU.subtract)\
                        .then_inc(rest_ready, 1)
                dve.wait_ge(rest_ready, count(rest_ready, b, 2 * side + 2))
                dve.tensor_copy(parts[1][:, 2 * side:2 * side + 2, :], rest[:, :, :]).then_inc(mid_ready, 1)

            def normalise(b, chain, ahead):
                dve.wait_ge(o_in_psum, count(o_in_psum, b, T))
                z = M[:, 0:T, :].rearrange("p t (h n) -> p t h n", n=32)[:, :, :, HD]
                chain.link(dve.tensor_scalar(den[:, :, :], z, DEN_EPS, None, ALU.add))
                chain.link(dve.reciprocal(rden[:, :, :], den[:, :, :]))
                if ahead:
                    dve.wait_ge(xn1T_in_psum, count(xn1T_in_psum, b + 1, KD))
                for t in range(T):
                    ins = dve.tensor_tensor(
                        tok[:, t, :].rearrange("p (h d) -> p h d", h=HEADS),
                        M[:, t, :].rearrange("p (h n) -> p h n", n=32)[:, :, 0:HD],
                        rden[:, t, :].unsqueeze(2).to_broadcast([P, HEADS, HD]), ALU.mult)
                ins.then_inc(o_normed, 1)

            def add_attention(b):
                dve.wait_ge(x_res_ready, count(x_res_ready, b, 16))
                for j in range(2):
                    dve.wait_ge(wo_in_psum, count(wo_in_psum, b, j + 1))
                    dve.tensor_tensor(x1[:, 2 * j:2 * j + 2, :].rearrange("p t d -> p (t d)"), M[:, 2 + j, :],
                                      x_res[:, 2 * j:2 * j + 2, :].rearrange("p t d -> p (t d)"), ALU.add)\
                        .then_inc(x1_ready, 1)

            def norm2(b, chain):
                dve.wait_ge(x1_ready, count(x1_ready, b, 2))
                norm_stats(chain, x1, st2, mv2, ve2, var2_ready)
                dve.wait_ge(rstd2_ready, count(rstd2_ready, b, 1))
                dve.wait_ge(onT_in_psum, count(onT_in_psum, b, KD))
                norm_apply(tok, x1, mv2, rs2).then_inc(xn2_ready, 1)

            def gate(b):
                for f in range(T):
                    dve.wait_ge(gelu_ready, count(gelu_ready, b, f + 1))
                    dve.tensor_tensor(gT[:, f, :], M[:, (0, 1, 4, 5)[f], :], gl[:, f % 2, :], ALU.mult)\
                        .then_inc(gated, 1)

            def add_mix(b):
                if due(c := count(out_ready, b, 0)):
                    dve.wait_ge(out_ready, c)
                for j in range(2):
                    dve.wait_ge(mix_in_psum, count(mix_in_psum, b, j + 1))
                    dve.tensor_tensor(x2[:, 2 * j:2 * j + 2, :].rearrange("p t d -> p (t d)"), M[:, 2 + j, :],
                                      x1[:, 2 * j:2 * j + 2, :].rearrange("p t d -> p (t d)"), ALU.add)\
                        .then_inc(x2_ready, 1)

            def ffn_stats(b, chain):
                dve.wait_ge(x2_ready, count(x2_ready, b, 2))
                norm_stats(chain, x2, st3, mv3, ve3, var3_ready)

            def scales(chain, mx, sc, sd, w):
                chain.link(dve.tensor_scalar(mx[:, :], mx[:, :], CLIP, None, ALU.max))
                chain.link(dve.reciprocal(sc[:, :], mx[:, :]))
                chain.link(dve.tensor_scalar(sc[:, :], sc[:, :], 127.0, None, ALU.mult))
                chain.link(dve.reciprocal(sd[:, :], sc[:, :]))
                return dve.tensor_scalar(sd[:, :], sd[:, :], wmean[:, w:w + 1], None, ALU.mult)

            def quantise(b, chain):
                dve.wait_ge(rstd3_ready, count(rstd3_ready, b, 1))
                dve.wait_ge(rows_free, count(rows_free, b, 16))
                chain.link(norm_apply(xn3, x2, mv3, rs3))
                chain.link(dve.tensor_reduce(mx3[:, :], xn3[:, :, :], AX.X, ALU.max, apply_absolute_value=True))
                chain.link(scales(chain, mx3, sc3, sdq, 0))
                for t in range(T):
                    ins = dve.tensor_scalar(xn3[:, t, :], xn3[:, t, :], sc3[:, t:t + 1], MAGIC, ALU.mult, ALU.add)
                chain.link(ins)
                dve.tensor_scalar(xq[:, :, :], xn3[:, :, :], -MAGIC, None, ALU.add).then_inc(xq_ready, 1)

            def up_scaled(b, f):
                dve.wait_ge(up_in_psum, count(up_in_psum, b, f + 1))
                if f == 0:
                    dve.wait_ge(sB_ready, count(sB_ready, b, 1))
                if f >= 2:
                    if due(c := count(conv_ready, b, f - 1)):
                        dve.wait_ge(conv_ready, c)
                dve.tensor_tensor(hs[:, f % 2, 1:L + 1], FB[:, f % 2, :], sB[:, :], ALU.mult)\
                    .then_inc(hs_ready, 1)

            def side_taps(b, f, chain):
                dve.wait_ge(centre_ready, count(centre_ready, b, f + 1))
                chain.link(dve.scalar_tensor_tensor(out=cv[:, f % 2, :], in0=hs[:, f % 2, 0:L], scalar=cw[:, f, 0:1],
                                                    in1=cv[:, f % 2, :], op0=ALU.mult, op1=ALU.add))
                dve.scalar_tensor_tensor(out=cv[:, f % 2, :], in0=hs[:, f % 2, 2:L + 2], scalar=cw[:, f, 2:3],
                                         in1=cv[:, f % 2, :], op0=ALU.mult, op1=ALU.add)\
                    .then_inc(conv_ready, 1)

            def ffn_conv(b, chain):
                for f in range(NF):
                    up_scaled(b, f)
                    if f >= 1:
                        side_taps(b, f - 1, chain)
                side_taps(b, NF - 1, chain)

            def hidden_max(b):
                dve.wait_ge(silu_ready, count(silu_ready, b, NF))
                dve.tensor_reduce(am[:, :], act_out[:, :, :].rearrange("p f t -> p t f"), AX.X, ALU.max,
                                  apply_absolute_value=True).then_inc(am_ready, 1)

            def hidden_scales(b):
                dve.wait_ge(amT_in_psum, count(amT_in_psum, b, 1))
                chain = Chain(dve, hidden_chain, b)
                chain.link(dve.tensor_reduce(mx4[:, :], FB[:, 0, :].rearrange("p (t n) -> p t n", t=T), AX.X, ALU.max))
                scales(chain, mx4, sc4, sdq4, 1).then_inc(s2_ready, 1)
                chain.end()

            def hidden_round(b):
                for j in range(NF // 2):
                    dve.wait_ge(scaled, count(scaled, b, 2 * j + 2))
                    dve.tensor_scalar(hq[:, 2 * j:2 * j + 2, :], act_out[:, 2 * j:2 * j + 2, :], MAGIC, -MAGIC,
                                      ALU.add, ALU.add).then_inc(hq_ready, 1)

            def finish(b):
                for t in range(T):
                    if t % 2 == 0:
                        dve.wait_ge(down_in_psum, count(down_in_psum, b, t // 2 + 1))
                    ins = dve.scalar_tensor_tensor(out=xn3[:, t, :], in0=FB[:, t // 2, (t % 2) * D:(t % 2 + 1) * D],
                                                   scalar=sdq4[:, t:t + 1], in1=x2[:, t, :],
                                                   op0=ALU.mult, op1=ALU.add)
                ins.then_inc(out_ready, 1)

            def quantise_weights():
                n = [0]

                def link(ins):
                    n[0] += 1
                    ins.then_inc(setup_dve, 1)
                    dve.wait_ge(setup_dve, n[0])

                dve.wait_ge(raw_loaded, 32)
                dve.tensor_reduce(wsum[:, 0:1], w_raw[:, 0:KD * F], AX.X, ALU.add, apply_absolute_value=True)
                dve.tensor_reduce(wsum[:, 1:2], w_raw[:, KD * F:2 * KD * F], AX.X, ALU.add,
                                  apply_absolute_value=True).then_inc(wsum_ready, 1)
                dve.wait_ge(wtotal_ready, 1)
                link(dve.tensor_scalar(wmean[:, :], FB[:, 0, 0:2], 1.0 / (D * F), CLIP, ALU.mult, ALU.max))
                link(dve.reciprocal(wscale[:, :], wmean[:, :]))
                for w, q in enumerate((w_up_q[:, :, :].rearrange("p k n -> p (k n)"),
                                       w_dn_q[:, :, :].rearrange("p f n -> p (f n)"))):
                    raw = w_raw[:, w * KD * F:(w + 1) * KD * F]
                    link(dve.tensor_scalar(raw, raw, wscale[:, w:w + 1], MAGIC, ALU.mult, ALU.add))
                    link(dve.tensor_scalar(raw, raw, -MAGIC, 1.0, ALU.add, ALU.min))
                    dve.tensor_scalar(q, raw, -1.0, None, ALU.max).then_inc(weights_quantised, 1)

            def iteration(b, ahead, behind):
                main = Chain(dve, main_chain, b)
                if behind:
                    ffn = Chain(dve, ffn_chain, b - 1)
                    ffn_stats(b - 1, ffn)
                if ahead:
                    pre_stats(b + 1)
                if behind:
                    quantise(b - 1, ffn)
                if ahead:
                    pre_norm(b + 1)
                if behind:
                    ffn_conv(b - 1, ffn)
                    ffn.end()
                    hidden_max(b - 1)
                elif ahead:
                    quantise_weights()
                normalise(b, main, ahead)
                if ahead:
                    split(b + 1, 0)
                if behind:
                    hidden_scales(b - 1)
                add_attention(b)
                norm2(b, main)
                main.end()
                if ahead:
                    split(b + 1, 1)
                gate(b)
                if behind:
                    hidden_round(b - 1)
                    finish(b - 1)
                add_mix(b)

            dve.wait_ge(consts_ready, 8)
            dve.tensor_copy(identb[:, :], ident[:, :]).then_inc(consts_ready, 1)
            pre_stats(0)
            pre_norm(0)
            split(0, 0)
            split(0, 1)
            dve.wait_ge(w_rest_loaded, 16 * 3)
            iteration(0, True, False)
            with dve.Fori(1, B - 1) as b:
                iteration(b, True, True)
            iteration(B - 1, False, True)
            last = B - 1
            ffn = Chain(dve, ffn_chain, last)
            ffn_stats(last, ffn)
            quantise(last, ffn)
            ffn_conv(last, ffn)
            ffn.end()
            hidden_max(last)
            hidden_scales(last)
            hidden_round(last)
            finish(last)

        @block.tensor
        def _(pe):
            def transpose_rows(src, bank, in_psum):
                for k in range(KD):
                    for t in range(T):
                        ins = pe.transpose(M[:, bank + k, t * P:(t + 1) * P], src[:, t, k * P:(k + 1) * P], ident[:, :])
                    ins.then_inc(in_psum, 1)

            def product(dst, pairs):
                for n, (lhsT, rhs) in enumerate(pairs):
                    ins = pe.matmul(dst, lhsT, rhs, start=(n == 0), stop=(n == len(pairs) - 1))
                return ins

            def xn1T(b):
                pe.wait_ge(xn1_ready, count(xn1_ready, b, 1))
                if due(c := count(oT_ready, b, 0)):
                    pe.wait_ge(oT_ready, c)
                transpose_rows(tok, 4, xn1T_in_psum)

            def qk(b, m):
                pe.wait_ge(xn1T_ready, count(xn1T_ready, b, KD))
                if due(c := count(rest_ready, b, m - 1)):
                    pe.wait_ge(rest_ready, c)
                product(M[:, 4 + m % 2, :], [(wqk[:, k, m * P:(m + 1) * P], norm1T[:, k, :]) for k in range(KD)])\
                    .then_inc(qk_in_psum, 1)

            def v(b):
                if due(c := count(onT_ready, b, 0)):
                    pe.wait_ge(onT_ready, c)
                for j in range(2):
                    for t in (2 * j, 2 * j + 1):
                        ins = product(M[:, j, (t % 2) * D:(t % 2 + 1) * D],
                                      [(norm1T[:, k, t * P:(t + 1) * P], wv[:, k, :]) for k in range(KD)])
                    ins.then_inc(v_in_psum, 1)

            def scores(b, g):
                for n in range(PIECES):
                    p = PIECES * g + n
                    if p == 0:
                        pe.wait_ge(spread, count(spread, b, per["spread"]))
                        pe.wait_ge(v_ready, count(v_ready, b, 2))
                        if due(c := count(gated, b, 0)):
                            pe.wait_ge(gated, c)
                    elif p == 1:
                        if due(c := count(x2_ready, b, 0)):
                            pe.wait_ge(x2_ready, c)
                    else:
                        if due(c := count(squared, b, p - 1)):
                            pe.wait_ge(squared, c)
                    lo = 2 * (p % 2)
                    if n < GROUP:
                        h = GROUP * g + n
                        q, k = Qs[:, h % HALF, h // HALF, :], Ks[:, h % HALF, h // HALF, :]
                        for j in (0, 1, 3):
                            at = TILE_AT[j]
                            ins = pe.matmul(M[:, lo + at // BANK, at % BANK:at % BANK + L - j * P],
                                            k[:, j * P:(j + 1) * P], q[:, j * P:L], start=True, stop=True)
                    else:
                        for a in range(GROUP):
                            h = GROUP * g + a
                            q, k = Qs[:, h % HALF, h // HALF, :], Ks[:, h % HALF, h // HALF, :]
                            at = a * 256
                            ins = pe.matmul(M[:, lo + at // BANK, at % BANK:at % BANK + 256],
                                            k[:, 2 * P:3 * P], q[:, 2 * P:L], start=True, stop=True)
                    ins.then_inc(scores_ready, 1)

            def values(b, g):
                pe.wait_ge(masked, count(masked, b, 3 * g + 3))
                if g < 2:
                    if due(c := count(gated, b, 0)):
                        pe.wait_ge(gated, c)
                    pe.wait_ge(rest_ready, count(rest_ready, b, 4))
                    pe.wait_ge(v_ready, count(v_ready, b, 2))
                else:
                    if due(c := count(oT_ready, b, g - 1)):
                        pe.wait_ge(oT_ready, c)
                for j in range(T):
                    for a in range(GROUP):
                        at = a * 1024 + TILE_AT[j] if j != 2 else TILE2_AT + a * 256
                        ins = pe.matmul(M[32 * a:32 * a + 32, 4 + g % 2, j * P:L], V1[:, j, GROUP * g + a, :],
                                        A[:, g % 2, at:at + L - j * P], start=(j == 0), stop=(j == T - 1))
                ins.then_inc(values_summed, 1)

            def o_rows(b):
                pe.wait_ge(squared, count(squared, b, NP))
                pe.wait_ge(oT_ready, count(oT_ready, b, GROUPS))
                for t in range(T):
                    for g in range(GROUPS):
                        ins = pe.transpose(M[:, t, g * P:(g + 1) * P], oT[:, g, t * P:(t + 1) * P], ident[:, :])
                    ins.then_inc(o_in_psum, 1)

            def onT(b):
                pe.wait_ge(o_normed, count(o_normed, b, 1))
                transpose_rows(tok, 0, onT_in_psum)

            def token_product(bank, lhs, rhs, n, in_psum):
                for j in range(2):
                    for t in (2 * j, 2 * j + 1):
                        ins = product(M[:, bank + j, (t % 2) * D:(t % 2 + 1) * D],
                                      [(lhs[:, k, t * P:(t + 1) * P], rhs[:, k, :]) for k in range(n)])
                    ins.then_inc(in_psum, 1)

            def wo_product(b):
                pe.wait_ge(onT_ready, count(onT_ready, b, KD))
                token_product(2, rowT, wo, KD, wo_in_psum)

            def xn2T(b):
                pe.wait_ge(xn2_ready, count(xn2_ready, b, 1))
                transpose_rows(tok, 2, xn2T_in_psum)

            def context_up(b, ahead):
                pe.wait_ge(ctx_loaded, count(ctx_loaded, b, 32))
                pe.wait_ge(xn2T_ready, count(xn2T_ready, b, KD))
                for f, bank in enumerate((0, 1, 4, 5)):
                    if f == 0 and ahead:
                        pe.wait_ge(v_ready, count(v_ready, b + 1, 2))
                    if f == 2 and ahead:
                        pe.wait_ge(rest_ready, count(rest_ready, b + 1, 4))
                    product(M[:, bank, :], [(ctxT[:, k, f * P:(f + 1) * P], rowT[:, k, :]) for k in range(KD)])\
                        .then_inc(h1_in_psum, 1)

            def context_down(b):
                pe.wait_ge(gated, count(gated, b, T))
                token_product(2, gT, ctxR, T, mix_in_psum)

            def xqT_and_scales(b):
                pe.wait_ge(xq_ready, count(xq_ready, b, 1))
                xqT_ps = FB[:, 0, :].bitcast(bf16)
                for k in range(KD):
                    for t in range(T):
                        ins = pe.transpose(xqT_ps[:, k * L + t * P:k * L + (t + 1) * P],
                                           xq[:, t, k * P:(k + 1) * P], identb[:, :])
                ins.then_inc(xqT_in_psum, 1)
                spread_scales(sdq).then_inc(s_in_psum, 1)

            def spread_scales(s):
                for t in range(T):
                    ins = pe.transpose(FB[:, 1, t * P:(t + 1) * P], s[:, t:t + 1].to_broadcast([P, P]), ident[:, :])
                return ins

            def ffn_up(b, f):
                if f == 0:
                    pe.wait_ge(xqT_ready, count(xqT_ready, b, 1))
                if f == 1:
                    pe.wait_ge(sB_ready, count(sB_ready, b, 1))
                if f >= 2:
                    if due(c := count(hs_ready, b, f - 1)):
                        pe.wait_ge(hs_ready, c)
                product(FB[:, f % 2, :], [(w_up_q[:, k, f * P:(f + 1) * P], xqT[:, k, :]) for k in range(KD)])\
                    .then_inc(up_in_psum, 1)

            def hidden_max_rows(b):
                pe.wait_ge(am_ready, count(am_ready, b, 1))
                pe.wait_ge(hs_ready, count(hs_ready, b, NF))
                for t in range(T):
                    ins = pe.transpose(FB[:, 0, t * P:(t + 1) * P], am[:, t * P:(t + 1) * P], ident[:, :])
                ins.then_inc(amT_in_psum, 1)

            def hidden_scales(b):
                pe.wait_ge(s2_ready, count(s2_ready, b, 1))
                spread_scales(sc4).then_inc(s2_in_psum, 1)

            def ffn_down(b):
                pe.wait_ge(s2B_ready, count(s2B_ready, b, 1))
                pe.wait_ge(hq_ready, count(hq_ready, b, NF // 2))
                for j in range(2):
                    for t in (2 * j, 2 * j + 1):
                        ins = product(FB[:, j, (t % 2) * D:(t % 2 + 1) * D],
                                      [(hq[:, f, t * P:(t + 1) * P], w_dn_q[:, f, :]) for f in range(NF)])
                    ins.then_inc(down_in_psum, 1)

            def weights_total():
                pe.wait_ge(wsum_ready, 1)
                pe.matmul(FB[:, 0, 0:2], ones[:, :], wsum[:, :], start=True, stop=True).then_inc(wtotal_ready, 1)

            def attention(b, behind):
                ups = iter(range(NF if behind else 0))

                def up(n):
                    for _ in range(n):
                        f = next(ups, None)
                        if f is not None:
                            ffn_up(b - 1, f)

                scores(b, 0)
                scores(b, 1)
                if behind:
                    xqT_and_scales(b - 1)
                values(b, 0)
                up(2)
                scores(b, 2)
                up(1)
                values(b, 1)
                up(2)
                scores(b, 3)
                up(1)
                values(b, 2)
                up(1)
                values(b, 3)
                up(1)
                if not behind:
                    weights_total()

            def iteration(b, ahead, behind):
                attention(b, behind)
                o_rows(b)
                if ahead:
                    xn1T(b + 1)
                    qk(b + 1, 0)
                    qk(b + 1, 1)
                onT(b)
                wo_product(b)
                if behind:
                    hidden_max_rows(b - 1)
                if ahead:
                    qk(b + 1, 2)
                    qk(b + 1, 3)
                if behind:
                    hidden_scales(b - 1)
                if ahead:
                    v(b + 1)
                xn2T(b)
                context_up(b, ahead)
                if behind:
                    ffn_down(b - 1)
                context_down(b)

            pe.wait_ge(consts_ready, 9)
            pe.wait_ge(w_qkv_loaded, 16 * 2)
            xn1T(0)
            for m in range(4):
                qk(0, m)
            v(0)
            pe.wait_ge(w_rest_loaded, 16 * 3)
            iteration(0, True, False)
            pe.wait_ge(weights_quantised, 2)
            with pe.Fori(1, B - 1) as b:
                iteration(b, True, True)
            iteration(B - 1, False, True)
            xqT_and_scales(B - 1)
            for f in range(NF):
                ffn_up(B - 1, f)
            hidden_max_rows(B - 1)
            hidden_scales(B - 1)
            ffn_down(B - 1)


def kernel(**inputs):
    import numpy as np
    import concourse.bacc as bacc
    from concourse.bass_utils import run_bass_kernel_spmd

    a = {n: np.asarray(v) for n, v in inputs.items()}
    D = a["x"].shape[2]
    H = 16
    P = 128

    def dims_outside_heads(w):
        return w.reshape(D, 2, H // 2, D // H).transpose(0, 1, 3, 2).reshape(D, D)

    conv_w = a["L0_ffn_conv_w"]
    arrays = {
        "x": a["x"],
        "ctx_rows": a["ctx_1024"],
        "ctx_cols": a["ctx_1024"].transpose(0, 2, 1),
        "w_qk": np.concatenate([dims_outside_heads(a["L0_attn_Wq"]), dims_outside_heads(a["L0_attn_Wk"])], axis=1),
        "w_v": a["L0_attn_Wv"],
        "w_o": a["L0_attn_Wo"],
        "w_up": a["L0_ffn_w1"].T,
        "conv_w": conv_w.reshape(-1, P, 3).transpose(1, 0, 2),
        "conv_b": a["L0_ffn_conv_b"].reshape(-1, P).T,
        "w_down": a["L0_ffn_w2"].T,
    }
    arrays = {n: np.ascontiguousarray(v) for n, v in arrays.items()}
    nc = bacc.Bacc("TRN2", target_bir_lowering=False, num_devices=1)
    args = [nc.dram_tensor(n, v.shape, mybir.dt.from_np(v.dtype), kind="ExternalInput").ap()
            for n, v in arrays.items()]
    out = nc.dram_tensor("out", a["x"].shape, mybir.dt.from_np(a["x"].dtype), kind="ExternalOutput").ap()
    decoder_layer(nc, *args, out)
    return run_bass_kernel_spmd(nc, [arrays], core_ids=[0]).results[0]["out"]
```

```python
import concourse.bass as bass
from concourse import mybir
from contextlib import ExitStack


def decoder_layer(nc, x, ctx_rows, ctx_cols, w_qk, w_v, w_o, w_up, conv_w, conv_b, w_down, out):
    fp32 = mybir.dt.float32
    bf16 = mybir.dt.bfloat16
    ALU = mybir.AluOpType
    ACT = mybir.ActivationFunctionType
    AX = mybir.AxisListType

    B, L, D = x.shape
    F = w_up.shape[1]
    P = 128
    T = L // P
    KD = D // P
    NF = F // P
    HEADS, HD = 16, 16
    GROUP = 4
    GROUPS = HEADS // GROUP
    HALF = HEADS // 2
    BANK = 512
    QSCALE = float(HD) ** -0.5
    LN_EPS = 1e-5
    DEN_EPS = 1e-5
    CLIP = 1e-5
    MAGIC = 12582912.0
    PIECES = GROUP + 1
    NP = GROUPS * PIECES
    TILE_AT = [0, 640, None, 512]
    TILE2_AT = GROUP * 1024

    Q_PART = [0, 0, 1, 1, 0, 2, 1, 2]
    K_PART = [0, 1, 0, 1, 2, 0, 2, 1]
    NG = len(Q_PART)

    with ExitStack() as stack:
        def sb(name, shape, dt=fp32):
            return stack.enter_context(nc.sbuf_tensor(name, shape, dt))

        def sem(name):
            return stack.enter_context(nc.semaphore(name))

        ident = sb("ident", [P, P])
        identb = sb("identb", [P, P], bf16)
        ones = sb("ones", [P, P])
        neg_half = sb("neg_half", [P, T])
        wqk = sb("wqk", [P, KD, 2 * D])
        wv = sb("wv", [P, KD, D])
        wo = sb("wo", [P, KD, D])
        w_up_q = sb("w_up_q", [P, KD, F], bf16)
        w_dn_q = sb("w_dn_q", [P, NF, D], bf16)
        cw = sb("cw", [P, NF, 3])
        cb = sb("cb", [P, NF])
        wsum = sb("wsum", [P, 2])
        wmean = sb("wmean", [P, 2])
        wscale = sb("wscale", [P, 2])

        x_in = sb("x_in", [P, T, D])
        tok = sb("tok", [P, T, D])
        norm1T = sb("norm1T", [P, KD, L])
        parts = [sb(f"part_{n}", [P, 4, L], bf16) for n in ("high", "mid", "low")]
        rest = sb("rest", [P, 2, L])
        Qs = sb("Qs", [P, HALF, 2, L], bf16)
        Ks = sb("Ks", [P, HALF, 2, L], bf16)
        V1 = sb("V1", [P, T, HEADS, 32])
        st1, mv1, ve1, rs1 = sb("st1", [P, T, 6]), sb("mv1", [P, T, 2]), sb("ve1", [P, T]), sb("rs1", [P, T])

        x_res = sb("x_res", [P, T, D])
        A = sb("A", [P, 2, GROUP * 1280])
        oT = sb("oT", [P, GROUPS, L])
        den = sb("den", [P, T, HEADS])
        rden = sb("rden", [P, T, HEADS])
        onT = sb("onT", [P, KD, L])
        x1 = sb("x1", [P, T, D])

        xn2 = sb("xn2", [P, T, D])
        xn2T = sb("xn2T", [P, KD, L])
        ctxT = sb("ctxT", [P, KD, L])
        ctxR = sb("ctxR", [P, T, D])
        gl = sb("gl", [P, L])
        gT = sb("gT", [P, T, L])
        x2 = sb("x2", [P, T, D])
        st2, mv2, ve2, rs2 = sb("st2", [P, T, 6]), sb("mv2", [P, T, 2]), sb("ve2", [P, T]), sb("rs2", [P, T])

        xn3 = sb("xn3", [P, T, D])
        xq = sb("xq", [P, T, D], bf16)
        xqT = sb("xqT", [P, KD, L], bf16)
        sB = sb("sB", [P, L])
        hs = sb("hs", [P, 2, L + 2])
        cv = sb("cv", [P, 2, L])
        act_out = sb("act_out", [P, NF, L])
        w_raw = act_out[:, :, :].rearrange("p f t -> p (f t)")
        am = sb("am", [P, L])
        s2B = sB
        hq = sb("hq", [P, NF, L], bf16)
        st3, mv3, ve3, rs3 = sb("st3", [P, T, 6]), sb("mv3", [P, T, 2]), sb("ve3", [P, T]), sb("rs3", [P, T])
        mx3, sc3, sdq = sb("mx3", [P, T]), sb("sc3", [P, T]), sb("sdq", [P, T])
        mx4, sc4, sdq4 = sb("mx4", [P, T]), sb("sc4", [P, T]), sb("sdq4", [P, T])

        psum = stack.enter_context(nc.psum_tensor("psum", [P, 8, BANK], fp32))
        sum_bank = psum[:, 4, :]
        att_bank = psum[:, 5, :]
        mix_bank = psum[:, 6, :]
        ffn_bank = psum[:, 7, :]

        per = {}

        def psem(name, n):
            per[name] = n
            return sem(name)

        w_qkv_loaded = sem("w_qkv_loaded")
        w_rest_loaded = sem("w_rest_loaded")
        waited = sem("waited")
        raw_loaded = sem("raw_loaded")
        consts_ready = sem("consts_ready")
        setup_dve = sem("setup_dve")
        wsum_ready = sem("wsum_ready")
        wtotal_ready = sem("wtotal_ready")
        weights_quantised = sem("weights_quantised")

        x_in_loaded = psem("x_in_loaded", 16)
        var1_ready = psem("var1_ready", 1)
        rstd1_ready = psem("rstd1_ready", 1)
        xn1_ready = psem("xn1_ready", 1)
        xn1T_in_psum = psem("xn1T_in_psum", KD)
        xn1T_ready = psem("xn1T_ready", KD)
        qk_in_psum = psem("qk_in_psum", 4)
        high_ready = psem("high_ready", 4)
        rest_ready = psem("rest_ready", 4)
        mid_ready = psem("mid_ready", 2)
        low_ready = psem("low_ready", 2)
        q_spread = psem("q_spread", NG * 16)
        k_spread = psem("k_spread", NG * 16)
        v_in_psum = psem("v_in_psum", 2)
        v_ready = psem("v_ready", 2)
        norm1_chain = psem("norm1_chain", 2)

        x_res_ready = psem("x_res_ready", 16)
        scores_ready = psem("scores_ready", NP)
        squared = psem("squared", NP)
        masked = psem("masked", 3 * GROUPS)
        values_summed = psem("values_summed", GROUPS)
        oT_ready = psem("oT_ready", GROUPS)
        o_in_psum = psem("o_in_psum", T)
        o_normed = psem("o_normed", T)
        onT_in_psum = psem("onT_in_psum", KD)
        onT_ready = psem("onT_ready", KD)
        wo_in_psum = psem("wo_in_psum", 2)
        x1_ready = psem("x1_ready", 2)
        divide_chain = psem("divide_chain", 2 * T)

        ctx_loaded = psem("ctx_loaded", 32)
        var2_ready = psem("var2_ready", 1)
        rstd2_ready = psem("rstd2_ready", 1)
        xn2_ready = psem("xn2_ready", 1)
        xn2T_in_psum = psem("xn2T_in_psum", KD)
        xn2T_ready = psem("xn2T_ready", KD)
        h1_in_psum = psem("h1_in_psum", T)
        gelu_ready = psem("gelu_ready", T)
        gated = psem("gated", T)
        mix_in_psum = psem("mix_in_psum", 2)
        x2_ready = psem("x2_ready", 2)
        norm2_chain = psem("norm2_chain", 2)

        var3_ready = psem("var3_ready", 1)
        rstd3_ready = psem("rstd3_ready", 1)
        xq_ready = psem("xq_ready", 1)
        xqT_in_psum = psem("xqT_in_psum", 1)
        xqT_ready = psem("xqT_ready", 1)
        s_in_psum = psem("s_in_psum", 1)
        sB_ready = psem("sB_ready", 1)
        up_in_psum = psem("up_in_psum", NF)
        hs_ready = psem("hs_ready", NF)
        centre_ready = psem("centre_ready", NF)
        conv_ready = psem("conv_ready", NF)
        silu_ready = psem("silu_ready", NF)
        am_ready = psem("am_ready", 2)
        amT_in_psum = psem("amT_in_psum", 1)
        s2_ready = psem("s2_ready", 1)
        s2_in_psum = psem("s2_in_psum", 1)
        s2B_ready = psem("s2B_ready", 1)
        scaled_on_pool = psem("scaled_on_pool", NF // 2)
        scaled_on_dve = psem("scaled_on_dve", NF // 2)
        hq_ready = psem("hq_ready", NF // 2)
        down_in_psum = psem("down_in_psum", 2)
        out_ready = psem("out_ready", 2)
        rows_stored = psem("rows_stored", 16)
        norm3_chain = psem("norm3_chain", 2)
        quantise_chain = psem("quantise_chain", 8)
        taps_chain = psem("taps_chain", NF)
        hidden_chain = psem("hidden_chain", 5)

        def count(s, b, n):
            return per[s.name] * b + n

        def due(value):
            return not isinstance(value, int) or value > 0

        def absent(b):
            return isinstance(b, int) and not 0 <= b < B

        def settle(eng):
            eng.sem_inc(waited, 1)

        class Chain:

            def __init__(self, eng, sem, b, n=0):
                self.eng, self.sem, self.b, self.n = eng, sem, b, n

            def link(self, ins):
                self.n += 1
                ins.then_inc(self.sem, 1)
                self.eng.wait_ge(self.sem, count(self.sem, self.b, self.n))

        def rows(dram, b):
            return dram[bass.ds(b, 1), :, :].rearrange("o (t p) d -> p (o t) d", p=P)

        block = stack.enter_context(nc.Block())

        @block.sync
        def _(sp):
            def load_x(b):
                if absent(b):
                    return
                if due(c := count(xn1_ready, b, 0)):
                    sp.wait_ge(xn1_ready, c)
                settle(sp)
                if due(c := count(x_res_ready, b, 0)):
                    sp.wait_ge(x_res_ready, c)
                settle(sp)
                sp.dma_start(x_in[:, :, :], rows(x, b)).then_inc(x_in_loaded, 16)

            def copy_x(b):
                if absent(b):
                    return
                sp.wait_ge(x_in_loaded, count(x_in_loaded, b, 16))
                if due(c := count(x1_ready, b, 0)):
                    sp.wait_ge(x1_ready, c)
                sp.dma_start(x_res[:, :, :], x_in[:, :, :]).then_inc(x_res_ready, 16)

            def load_ctx(b):
                if absent(b):
                    return
                if due(c := count(mix_in_psum, b, 0)):
                    sp.wait_ge(mix_in_psum, c)
                settle(sp)
                sp.dma_start(ctxT[:, :, :], ctx_cols[bass.ds(b, 1), :, :].rearrange(
                    "o (k p) t -> p (o k) t", p=P)).then_inc(ctx_loaded, 16)
                sp.dma_start(ctxR[:, :, :], rows(ctx_rows, b)).then_inc(ctx_loaded, 16)

            def spread_side(b, side):
                if absent(b):
                    return
                dst, which, spread = ((Qs, Q_PART, q_spread), (Ks, K_PART, k_spread))[side]
                if due(c := count(scores_ready, b, 0)):
                    sp.wait_ge(scores_ready, c)
                settle(sp)
                for part, ready, n in ((0, high_ready, 2), (1, mid_ready, 1), (2, low_ready, 1)):
                    sp.wait_ge(ready, count(ready, b, n * (side + 1)))
                    for g in range(NG):
                        if which[g] == part:
                            sp.dma_start(dst[16 * g:16 * g + 16, :, :, :].rearrange("d h m t -> d (h m t)"),
                                         parts[part][:, 2 * side:2 * side + 2, :].rearrange("p m t -> p (m t)")
                                         ).then_inc(spread, 16)

            def store(b):
                if absent(b):
                    return
                sp.wait_ge(out_ready, count(out_ready, b, 2))
                settle(sp)
                sp.dma_start(rows(out, b), xn3[:, :, :]).then_inc(rows_stored, 16)

            def load_weights():
                sp.dma_start(wqk[:, :, :], w_qk.rearrange("(k p) n -> p k n", p=P)).then_inc(w_qkv_loaded, 16)
                sp.dma_start(wv[:, :, :], w_v.rearrange("(k p) n -> p k n", p=P)).then_inc(w_qkv_loaded, 16)
                sp.dma_start(wo[:, :, :], w_o.rearrange("(k p) n -> p k n", p=P)).then_inc(w_rest_loaded, 16)
                sp.dma_start(cw[:, :, :], conv_w).then_inc(w_rest_loaded, 16)
                sp.dma_start(cb[:, :], conv_b).then_inc(w_rest_loaded, 16)

            def load_ffn_weights():
                sp.dma_start(w_raw[:, 0:KD * F].rearrange("p (k n) -> p k n", k=KD),
                             w_up.rearrange("(k p) n -> p k n", p=P)).then_inc(raw_loaded, 16)
                sp.dma_start(w_raw[:, KD * F:2 * KD * F].rearrange("p (f n) -> p f n", f=NF),
                             w_down.rearrange("(f p) n -> p f n", p=P)).then_inc(raw_loaded, 16)

            def iteration(i, first=False):
                load_x(i)
                if first:
                    load_weights()
                store(i - 3)
                load_ctx(i - 1)
                spread_side(i, 0)
                spread_side(i, 1)
                if first:
                    load_ffn_weights()
                copy_x(i)

            iteration(0, first=True)
            iteration(1)
            iteration(2)
            with sp.Fori(3, B) as i:
                iteration(i)
            for i in range(B, B + 3):
                iteration(i)
            sp.wait_ge(rows_stored, 16 * B)

        @block.gpsimd
        def _(pool):
            def rstd(b, var_ready, ve, rs, ready):
                if absent(b):
                    return
                pool.wait_ge(var_ready, count(var_ready, b, 1))
                pool.tensor_tensor(rs[:, :], ve[:, :], neg_half[:, :], ALU.pow).then_inc(ready, 1)

            def rstd1(b):
                rstd(b, var1_ready, ve1, rs1, rstd1_ready)

            def rstd2(b):
                rstd(b, var2_ready, ve2, rs2, rstd2_ready)

            def rstd3(b):
                rstd(b, var3_ready, ve3, rs3, rstd3_ready)

            def mask_first(b, g):
                if absent(b):
                    return
                pool.wait_ge(squared, count(squared, b, PIECES * g + GROUP))
                settle(pool)
                first = A[:, g % 2, 0:TILE2_AT].rearrange("p (h n) -> p h n", h=GROUP)[:, :, 0:P]
                pool.affine_select(out=first, in_=first, compare_op=ALU.is_ge, fill=0.0, base=0,
                                   pattern=[[0, GROUP], [1, P]], channel_multiplier=-1).then_inc(masked, 1)

            def mask_pair(b, g):
                if absent(b):
                    return
                pair = A[:, g % 2, 0:TILE2_AT].rearrange("p (h n) -> p h n", h=GROUP)[
                    :, :, TILE_AT[3]:TILE_AT[3] + 2 * P].rearrange("p h (j c) -> p h j c", j=2)
                pool.affine_select(out=pair, in_=pair, compare_op=ALU.is_ge, fill=0.0, base=0,
                                   pattern=[[0, GROUP], [0, 2], [1, P]], channel_multiplier=-1).then_inc(masked, 1)

            def mask_last(b, g):
                if absent(b):
                    return
                pool.wait_ge(squared, count(squared, b, PIECES * g + PIECES))
                settle(pool)
                second = A[:, g % 2, TILE2_AT:TILE2_AT + 1024].rearrange("p (h n) -> p h n", h=GROUP)[:, :, 0:P]
                pool.affine_select(out=second, in_=second, compare_op=ALU.is_ge, fill=0.0, base=0,
                                   pattern=[[0, GROUP], [1, P]], channel_multiplier=-1).then_inc(masked, 1)

            def low_part(b, side):
                if absent(b):
                    return
                pool.wait_ge(rest_ready, count(rest_ready, b, 2 * side + 2))
                pool.wait_ge(mid_ready, count(mid_ready, b, side + 1))
                pool.tensor_tensor(parts[2][:, 2 * side:2 * side + 2, :], rest[:, :, :],
                                   parts[1][:, 2 * side:2 * side + 2, :], ALU.subtract).then_inc(low_ready, 1)

            def scale_hidden(b):
                if absent(b):
                    return
                pool.wait_ge(s2B_ready, count(s2B_ready, b, 1))
                for f in range(NF // 2):
                    pool.tensor_tensor(act_out[:, f, :], act_out[:, f, :], s2B[:, :], ALU.mult)\
                        .then_inc(scaled_on_pool, 1)

            def iteration(i):
                mask_pair(i - 1, 0)
                mask_last(i - 1, 0)
                rstd1(i)
                mask_first(i - 1, 1)
                mask_pair(i - 1, 1)
                mask_last(i - 1, 1)
                mask_first(i - 1, 2)
                mask_pair(i - 1, 2)
                scale_hidden(i - 3)
                mask_last(i - 1, 2)
                low_part(i, 0)
                mask_first(i - 1, 3)
                mask_pair(i - 1, 3)
                rstd3(i - 2)
                mask_last(i - 1, 3)
                low_part(i, 1)
                mask_first(i, 0)
                rstd2(i - 1)

            pool.memset(ident[:, :], 0.0).then_inc(consts_ready, 1)
            pool.memset(ones[:, :], 1.0).then_inc(consts_ready, 1)
            pool.memset(neg_half[:, :], -0.5).then_inc(consts_ready, 1)
            pool.wait_ge(consts_ready, 3)
            pool.affine_select(out=ident[:, :], in_=ident[:, :], compare_op=ALU.not_equal, fill=1.0,
                               base=0, pattern=[[-1, P]], channel_multiplier=1).then_inc(consts_ready, 1)
            pool.memset(V1[:, :, :, HD:32], 0.0).then_inc(consts_ready, 1)
            pool.wait_ge(consts_ready, 5)
            pool.memset(V1[:, :, :, HD:HD + 1], 1.0).then_inc(consts_ready, 1)
            pool.memset(hs[:, :, 0:1], 0.0).then_inc(consts_ready, 1)
            pool.memset(hs[:, :, L + 1:L + 2], 0.0).then_inc(consts_ready, 1)
            for i in range(3):
                iteration(i)
            with pool.Fori(3, B) as i:
                iteration(i)
            for i in range(B, B + 3):
                iteration(i)

        @block.scalar
        def _(act):
            def xn1T_copy(b, k):
                if absent(b):
                    return
                act.wait_ge(xn1T_in_psum, count(xn1T_in_psum, b, k + 1))
                act.activation(norm1T[:, k, :], att_bank, ACT.Copy).then_inc(xn1T_ready, 1)

            def high_part(b, m):
                if absent(b):
                    return
                act.wait_ge(qk_in_psum, count(qk_in_psum, b, m + 1))
                if m == 0:
                    if due(c := count(q_spread, b, 0)):
                        act.wait_ge(q_spread, c)
                if m == 2:
                    if due(c := count(k_spread, b, 0)):
                        act.wait_ge(k_spread, c)
                act.activation(parts[0][:, m, :], att_bank, ACT.Copy).then_inc(high_ready, 1)

            def v_copy(b, j):
                if absent(b):
                    return
                act.wait_ge(v_in_psum, count(v_in_psum, b, j + 1))
                if j == 0:
                    if due(c := count(values_summed, b, 0)):
                        act.wait_ge(values_summed, c)
                act.activation(V1[:, 2 * j:2 * j + 2, :, 0:HD],
                               att_bank.rearrange("p (t h d) -> p t h d", t=2, h=HEADS),
                               ACT.Copy).then_inc(v_ready, 1)

            def square(b, *pieces):
                if absent(b):
                    return
                for p in pieces:
                    g, n = p // PIECES, p % PIECES
                    act.wait_ge(scores_ready, count(scores_ready, b, p + 1))
                    if n == 0:
                        if due(c := count(values_summed, b, g - 1)):
                            act.wait_ge(values_summed, c)
                    act.activation(A[:, g % 2, n * 1024:(n + 1) * 1024],
                                   psum[:, 2 * (p % 2):2 * (p % 2) + 2, :].rearrange("p a n -> p (a n)"),
                                   ACT.Square, scale=QSCALE).then_inc(squared, 1)

            def oT_copy(b, g):
                if absent(b):
                    return
                act.wait_ge(values_summed, count(values_summed, b, g + 1))
                if g == 0:
                    if due(c := count(o_in_psum, b, 0)):
                        act.wait_ge(o_in_psum, c)
                act.activation(oT[:, g, :], sum_bank, ACT.Copy).then_inc(oT_ready, 1)

            def onT_copy(b, k):
                if absent(b):
                    return
                act.wait_ge(onT_in_psum, count(onT_in_psum, b, k + 1))
                act.activation(onT[:, k, :], att_bank, ACT.Copy).then_inc(onT_ready, 1)

            def xn2T_copy(b, k):
                if absent(b):
                    return
                act.wait_ge(xn2T_in_psum, count(xn2T_in_psum, b, k + 1))
                act.activation(xn2T[:, k, :], mix_bank, ACT.Copy).then_inc(xn2T_ready, 1)

            def gelu(b, f):
                if absent(b):
                    return
                act.wait_ge(h1_in_psum, count(h1_in_psum, b, f + 1))
                act.activation(gl[:, :], mix_bank, ACT.Gelu).then_inc(gelu_ready, 1)

            def xqT_copy(b):
                if absent(b):
                    return
                act.wait_ge(xqT_in_psum, count(xqT_in_psum, b, 1))
                act.activation(xqT[:, :, :].rearrange("p k t -> p (k t)"), ffn_bank.bitcast(bf16), ACT.Copy)\
                    .then_inc(xqT_ready, 1)

            def sB_copy(b):
                if absent(b):
                    return
                act.wait_ge(s_in_psum, count(s_in_psum, b, 1))
                act.activation(sB[:, :], ffn_bank, ACT.Copy).then_inc(sB_ready, 1)

            def centre_tap(b, f):
                if absent(b):
                    return
                act.wait_ge(hs_ready, count(hs_ready, b, f + 1))
                if f >= 2:
                    act.wait_ge(silu_ready, count(silu_ready, b, f - 1))
                act.activation(cv[:, f % 2, :], hs[:, f % 2, 1:L + 1], ACT.Identity,
                               scale=cw[:, f, 1:2], bias=cb[:, f:f + 1]).then_inc(centre_ready, 1)

            def silu(b, f):
                if absent(b):
                    return
                act.wait_ge(conv_ready, count(conv_ready, b, f + 1))
                act.activation(act_out[:, f, :], cv[:, f % 2, :], ACT.Silu).then_inc(silu_ready, 1)

            def s2B_copy(b):
                if absent(b):
                    return
                act.wait_ge(s2_in_psum, count(s2_in_psum, b, 1))
                act.activation(s2B[:, :], ffn_bank, ACT.Copy).then_inc(s2B_ready, 1)

            def iteration(i):
                centre_tap(i - 3, 5)
                square(i - 1, 5)
                silu(i - 3, 4)
                square(i - 1, 6)
                centre_tap(i - 3, 6)
                xn2T_copy(i - 2, 0)
                silu(i - 3, 5)
                square(i - 1, 7)
                xn2T_copy(i - 2, 1)
                centre_tap(i - 3, 7)
                silu(i - 3, 6)
                v_copy(i - 1, 1)
                square(i - 1, 8, 9)
                silu(i - 3, 7)
                oT_copy(i - 1, 0)
                square(i - 1, 10)
                gelu(i - 2, 0)
                square(i - 1, 11)
                xn1T_copy(i, 0)
                oT_copy(i - 1, 1)
                xn1T_copy(i, 1)
                square(i - 1, 12, 13)
                gelu(i - 2, 1)
                s2B_copy(i - 3)
                high_part(i, 0)
                gelu(i - 2, 2)
                square(i - 1, 14, 15)
                high_part(i, 1)
                square(i - 1, 16)
                gelu(i - 2, 3)
                square(i - 1, 17, 18)
                high_part(i, 2)
                square(i - 1, 19)
                oT_copy(i - 1, 2)
                high_part(i, 3)
                oT_copy(i - 1, 3)
                xqT_copy(i - 2)
                sB_copy(i - 2)
                centre_tap(i - 2, 0)
                onT_copy(i - 1, 0)
                centre_tap(i - 2, 1)
                onT_copy(i - 1, 1)
                silu(i - 2, 0)
                silu(i - 2, 1)
                centre_tap(i - 2, 2)
                square(i, 0)
                centre_tap(i - 2, 3)
                silu(i - 2, 2)
                square(i, 1)
                silu(i - 2, 3)
                centre_tap(i - 2, 4)
                square(i, 2, 3)
                v_copy(i, 0)
                square(i, 4)

            for i in range(3):
                iteration(i)
            with act.Fori(3, B) as i:
                iteration(i)
            for i in range(B, B + 3):
                iteration(i)

        @block.vector
        def _(dve):
            def norm_stats(chain, src, st, mv, ve, var_ready):
                for t in range(T):
                    ins = dve.bn_stats(st[:, t, :], src[:, t, :])
                chain.link(ins)
                settle(dve)
                for t in range(T):
                    ins = dve.bn_aggr(mv[:, t, :], st[:, t, :])
                chain.link(ins)
                dve.tensor_scalar(ve[:, :], mv[:, :, 1], LN_EPS, None, ALU.add).then_inc(var_ready, 1)

            def norm_apply(dst, src, mv, rs):
                for t in range(T):
                    ins = dve.tensor_scalar(dst[:, t, :], src[:, t, :], mv[:, t, 0:1], rs[:, t:t + 1],
                                            ALU.subtract, ALU.mult)
                return ins

            def stats1(b):
                if absent(b):
                    return
                dve.wait_ge(x_in_loaded, count(x_in_loaded, b, 16))
                norm_stats(Chain(dve, norm1_chain, b), x_in, st1, mv1, ve1, var1_ready)

            def norm1(b):
                if absent(b):
                    return
                dve.wait_ge(rstd1_ready, count(rstd1_ready, b, 1))
                if due(c := count(onT_in_psum, b, -KD)):
                    dve.wait_ge(onT_in_psum, c)
                norm_apply(tok, x_in, mv1, rs1).then_inc(xn1_ready, 1)

            def rest_part(b, m):
                if absent(b):
                    return
                dve.wait_ge(high_ready, count(high_ready, b, m + 1))
                if due(c := count(low_ready, b, m // 2)):
                    dve.wait_ge(low_ready, c)
                dve.tensor_tensor(rest[:, m % 2, :], att_bank, parts[0][:, m, :], ALU.subtract)\
                    .then_inc(rest_ready, 1)

            def mid_part(b, side):
                if absent(b):
                    return
                dve.wait_ge(rest_ready, count(rest_ready, b, 2 * side + 2))
                dve.tensor_copy(parts[1][:, 2 * side:2 * side + 2, :], rest[:, :, :]).then_inc(mid_ready, 1)

            def divide(b, t):
                if absent(b):
                    return
                dve.wait_ge(o_in_psum, count(o_in_psum, b, t + 1))
                chain = Chain(dve, divide_chain, b, 2 * t)
                sums = att_bank.rearrange("p (h n) -> p h n", n=32)
                chain.link(dve.tensor_scalar(den[:, t, :], sums[:, :, HD], DEN_EPS, None, ALU.add))
                chain.link(dve.reciprocal(rden[:, t, :], den[:, t, :]))
                if t == 0 and not absent(b + 1):
                    dve.wait_ge(xn1T_in_psum, count(xn1T_in_psum, b + 1, KD))
                dve.tensor_tensor(tok[:, t, :].rearrange("p (h d) -> p h d", h=HEADS), sums[:, :, 0:HD],
                                  rden[:, t, :].unsqueeze(2).to_broadcast([P, HEADS, HD]), ALU.mult)\
                    .then_inc(o_normed, 1)

            def add_attention(b, j):
                if absent(b):
                    return
                if j == 0:
                    dve.wait_ge(x_res_ready, count(x_res_ready, b, 16))
                dve.wait_ge(wo_in_psum, count(wo_in_psum, b, j + 1))
                dve.tensor_tensor(x1[:, 2 * j:2 * j + 2, :].rearrange("p t d -> p (t d)"), att_bank,
                                  x_res[:, 2 * j:2 * j + 2, :].rearrange("p t d -> p (t d)"), ALU.add)\
                    .then_inc(x1_ready, 1)

            def stats2(b):
                if absent(b):
                    return
                dve.wait_ge(x1_ready, count(x1_ready, b, 2))
                norm_stats(Chain(dve, norm2_chain, b), x1, st2, mv2, ve2, var2_ready)

            def norm2(b):
                if absent(b):
                    return
                dve.wait_ge(rstd2_ready, count(rstd2_ready, b, 1))
                norm_apply(xn2, x1, mv2, rs2).then_inc(xn2_ready, 1)

            def gate(b, f):
                if absent(b):
                    return
                dve.wait_ge(gelu_ready, count(gelu_ready, b, f + 1))
                dve.tensor_tensor(gT[:, f, :], mix_bank, gl[:, :], ALU.mult).then_inc(gated, 1)

            def add_mix(b, j):
                if absent(b):
                    return
                if j == 0:
                    if due(c := count(out_ready, b, 0)):
                        dve.wait_ge(out_ready, c)
                dve.wait_ge(mix_in_psum, count(mix_in_psum, b, j + 1))
                dve.tensor_tensor(x2[:, 2 * j:2 * j + 2, :].rearrange("p t d -> p (t d)"), mix_bank,
                                  x1[:, 2 * j:2 * j + 2, :].rearrange("p t d -> p (t d)"), ALU.add)\
                    .then_inc(x2_ready, 1)

            def stats3(b):
                if absent(b):
                    return
                dve.wait_ge(x2_ready, count(x2_ready, b, 2))
                norm_stats(Chain(dve, norm3_chain, b), x2, st3, mv3, ve3, var3_ready)

            def scales(chain, mx, sc, sd, w):
                chain.link(dve.tensor_scalar(mx[:, :], mx[:, :], CLIP, None, ALU.max))
                chain.link(dve.reciprocal(sc[:, :], mx[:, :]))
                chain.link(dve.tensor_scalar(sc[:, :], sc[:, :], 127.0, None, ALU.mult))
                chain.link(dve.reciprocal(sd[:, :], sc[:, :]))
                return dve.tensor_scalar(sd[:, :], sd[:, :], wmean[:, w:w + 1], None, ALU.mult)

            def norm3_max(b):
                if absent(b):
                    return
                dve.wait_ge(rstd3_ready, count(rstd3_ready, b, 1))
                if due(c := count(rows_stored, b, 0)):
                    dve.wait_ge(rows_stored, c)
                chain = Chain(dve, quantise_chain, b)
                chain.link(norm_apply(xn3, x2, mv3, rs3))
                chain.link(dve.tensor_reduce(mx3[:, :], xn3[:, :, :], AX.X, ALU.max, apply_absolute_value=True))

            def token_scales(b):
                if absent(b):
                    return
                chain = Chain(dve, quantise_chain, b, 2)
                chain.link(scales(chain, mx3, sc3, sdq, 0))

            def quantise_rows(b):
                if absent(b):
                    return
                chain = Chain(dve, quantise_chain, b, 7)
                for t in range(T):
                    ins = dve.tensor_scalar(xn3[:, t, :], xn3[:, t, :], sc3[:, t:t + 1], MAGIC, ALU.mult, ALU.add)
                chain.link(ins)
                dve.tensor_scalar(xq[:, :, :], xn3[:, :, :], -MAGIC, None, ALU.add).then_inc(xq_ready, 1)

            def up_scaled(b, f):
                if absent(b):
                    return
                dve.wait_ge(up_in_psum, count(up_in_psum, b, f + 1))
                if f == 0:
                    dve.wait_ge(sB_ready, count(sB_ready, b, 1))
                if f >= 2:
                    dve.wait_ge(conv_ready, count(conv_ready, b, f - 1))
                dve.tensor_tensor(hs[:, f % 2, 1:L + 1], ffn_bank, sB[:, :], ALU.mult).then_inc(hs_ready, 1)

            def side_taps(b, f):
                if absent(b):
                    return
                dve.wait_ge(centre_ready, count(centre_ready, b, f + 1))
                Chain(dve, taps_chain, b, f).link(
                    dve.scalar_tensor_tensor(out=cv[:, f % 2, :], in0=hs[:, f % 2, 0:L], scalar=cw[:, f, 0:1],
                                             in1=cv[:, f % 2, :], op0=ALU.mult, op1=ALU.add))
                dve.scalar_tensor_tensor(out=cv[:, f % 2, :], in0=hs[:, f % 2, 2:L + 2], scalar=cw[:, f, 2:3],
                                         in1=cv[:, f % 2, :], op0=ALU.mult, op1=ALU.add)\
                    .then_inc(conv_ready, 1)

            def hidden_max(b):
                if absent(b):
                    return
                dve.wait_ge(silu_ready, count(silu_ready, b, NF))
                for half in (slice(0, L // 2), slice(L // 2, L)):
                    dve.tensor_reduce(am[:, half], act_out[:, :, half].rearrange("p f t -> p t f"), AX.X, ALU.max,
                                      apply_absolute_value=True).then_inc(am_ready, 1)

            def hidden_scales(b):
                if absent(b):
                    return
                dve.wait_ge(amT_in_psum, count(amT_in_psum, b, 1))
                chain = Chain(dve, hidden_chain, b)
                chain.link(dve.tensor_reduce(mx4[:, :], ffn_bank.rearrange("p (t n) -> p t n", t=T), AX.X, ALU.max))
                scales(chain, mx4, sc4, sdq4, 1).then_inc(s2_ready, 1)

            def scale_hidden(b, f):
                if absent(b):
                    return
                dve.wait_ge(s2B_ready, count(s2B_ready, b, 1))
                dve.tensor_tensor(act_out[:, f, :], act_out[:, f, :], s2B[:, :], ALU.mult).then_inc(scaled_on_dve, 1)

            def hidden_round(b, j):
                if absent(b):
                    return
                if j < NF // 4:
                    dve.wait_ge(scaled_on_pool, count(scaled_on_pool, b, 2 * j + 2))
                else:
                    dve.wait_ge(scaled_on_dve, count(scaled_on_dve, b, 2 * j + 2 - NF // 2))
                dve.tensor_scalar(hq[:, 2 * j:2 * j + 2, :], act_out[:, 2 * j:2 * j + 2, :], MAGIC, -MAGIC,
                                  ALU.add, ALU.add).then_inc(hq_ready, 1)

            def finish(b, j):
                if absent(b):
                    return
                dve.wait_ge(down_in_psum, count(down_in_psum, b, j + 1))
                for t in (2 * j, 2 * j + 1):
                    ins = dve.scalar_tensor_tensor(out=xn3[:, t, :], in0=ffn_bank[:, (t % 2) * D:(t % 2 + 1) * D],
                                                   scalar=sdq4[:, t:t + 1], in1=x2[:, t, :],
                                                   op0=ALU.mult, op1=ALU.add)
                ins.then_inc(out_ready, 1)

            def sum_weights():
                dve.wait_ge(raw_loaded, 32)
                dve.tensor_reduce(wsum[:, 0:1], w_raw[:, 0:KD * F], AX.X, ALU.add, apply_absolute_value=True)
                dve.tensor_reduce(wsum[:, 1:2], w_raw[:, KD * F:2 * KD * F], AX.X, ALU.add,
                                  apply_absolute_value=True).then_inc(wsum_ready, 1)

            def quantise_weights():
                n = [0]

                def link(ins):
                    n[0] += 1
                    ins.then_inc(setup_dve, 1)
                    dve.wait_ge(setup_dve, n[0])

                dve.wait_ge(wtotal_ready, 1)
                link(dve.tensor_scalar(wmean[:, :], ffn_bank[:, 0:2], 1.0 / (D * F), CLIP, ALU.mult, ALU.max))
                link(dve.reciprocal(wscale[:, :], wmean[:, :]))
                for w, q in enumerate((w_up_q[:, :, :].rearrange("p k n -> p (k n)"),
                                       w_dn_q[:, :, :].rearrange("p f n -> p (f n)"))):
                    raw = w_raw[:, w * KD * F:(w + 1) * KD * F]
                    link(dve.tensor_scalar(raw, raw, wscale[:, w:w + 1], MAGIC, ALU.mult, ALU.add))
                    link(dve.tensor_scalar(raw, raw, -MAGIC, 1.0, ALU.add, ALU.min))
                    dve.tensor_scalar(q, raw, -1.0, None, ALU.max).then_inc(weights_quantised, 1)

            def iteration(i, second=False):
                norm2(i - 2)
                up_scaled(i - 3, 6)
                side_taps(i - 3, 5)
                side_taps(i - 3, 6)
                up_scaled(i - 3, 7)
                stats1(i)
                side_taps(i - 3, 7)
                norm1(i)
                if second:
                    quantise_weights()
                hidden_max(i - 3)
                gate(i - 2, 0)
                hidden_scales(i - 3)
                gate(i - 2, 1)
                scale_hidden(i - 3, 4)
                scale_hidden(i - 3, 5)
                scale_hidden(i - 3, 6)
                hidden_round(i - 3, 2)
                scale_hidden(i - 3, 7)
                rest_part(i, 0)
                hidden_round(i - 3, 3)
                hidden_round(i - 3, 0)
                hidden_round(i - 3, 1)
                gate(i - 2, 2)
                rest_part(i, 1)
                mid_part(i, 0)
                finish(i - 3, 0)
                gate(i - 2, 3)
                finish(i - 3, 1)
                add_mix(i - 2, 0)
                add_mix(i - 2, 1)
                stats3(i - 2)
                rest_part(i, 2)
                norm3_max(i - 2)
                token_scales(i - 2)
                rest_part(i, 3)
                quantise_rows(i - 2)
                divide(i - 1, 0)
                mid_part(i, 1)
                divide(i - 1, 1)
                divide(i - 1, 2)
                up_scaled(i - 2, 0)
                divide(i - 1, 3)
                up_scaled(i - 2, 1)
                side_taps(i - 2, 0)
                side_taps(i - 2, 1)
                up_scaled(i - 2, 2)
                add_attention(i - 1, 0)
                up_scaled(i - 2, 3)
                side_taps(i - 2, 2)
                side_taps(i - 2, 3)
                up_scaled(i - 2, 4)
                add_attention(i - 1, 1)
                stats2(i - 1)
                up_scaled(i - 2, 5)
                side_taps(i - 2, 4)

            dve.wait_ge(consts_ready, 8)
            dve.tensor_copy(identb[:, :], ident[:, :]).then_inc(consts_ready, 1)
            iteration(0)
            sum_weights()
            dve.wait_ge(w_rest_loaded, 16 * 3)
            iteration(1, second=True)
            iteration(2)
            with dve.Fori(3, B) as i:
                iteration(i)
            for i in range(B, B + 3):
                iteration(i)

        @block.tensor
        def _(pe):
            def product(dst, pairs):
                for n, (lhsT, rhs) in enumerate(pairs):
                    ins = pe.matmul(dst, lhsT, rhs, start=(n == 0), stop=(n == len(pairs) - 1))
                return ins

            def transpose_rows(bank, src, k):
                for t in range(T):
                    ins = pe.transpose(bank[:, t * P:(t + 1) * P], src[:, t, k * P:(k + 1) * P], ident[:, :])
                return ins

            def token_product(bank, j, lhs, rhs, n):
                for t in (2 * j, 2 * j + 1):
                    ins = product(bank[:, (t % 2) * D:(t % 2 + 1) * D],
                                  [(lhs[:, k, t * P:(t + 1) * P], rhs[:, k, :]) for k in range(n)])
                return ins

            def norm1_transpose(b, k):
                if absent(b):
                    return
                if k == 0:
                    pe.wait_ge(xn1_ready, count(xn1_ready, b, 1))
                    if due(c := count(v_ready, b, 0)):
                        pe.wait_ge(v_ready, c)
                else:
                    pe.wait_ge(xn1T_ready, count(xn1T_ready, b, k))
                transpose_rows(att_bank, tok, k).then_inc(xn1T_in_psum, 1)

            def qk(b, m):
                if absent(b):
                    return
                if m == 0:
                    pe.wait_ge(xn1T_ready, count(xn1T_ready, b, KD))
                else:
                    pe.wait_ge(rest_ready, count(rest_ready, b, m))
                product(att_bank, [(wqk[:, k, m * P:(m + 1) * P], norm1T[:, k, :]) for k in range(KD)])\
                    .then_inc(qk_in_psum, 1)

            def v(b, j):
                if absent(b):
                    return
                if j == 0:
                    if due(c := count(x1_ready, b, 0)):
                        pe.wait_ge(x1_ready, c)
                else:
                    pe.wait_ge(v_ready, count(v_ready, b, 1))
                token_product(att_bank, j, norm1T, wv, KD).then_inc(v_in_psum, 1)

            def scores(b, *pieces):
                if absent(b):
                    return
                for p in pieces:
                    g, n = p // PIECES, p % PIECES
                    if p == 0:
                        pe.wait_ge(q_spread, count(q_spread, b, per["q_spread"]))
                        pe.wait_ge(k_spread, count(k_spread, b, per["k_spread"]))
                    if due(c := count(squared, b, p - 1)):
                        pe.wait_ge(squared, c)
                    lo = 2 * (p % 2)
                    if n < GROUP:
                        h = GROUP * g + n
                        q, k = Qs[:, h % HALF, h // HALF, :], Ks[:, h % HALF, h // HALF, :]
                        for j in (0, 1, 3):
                            at = TILE_AT[j]
                            ins = pe.matmul(psum[:, lo + at // BANK, at % BANK:at % BANK + L - j * P],
                                            k[:, j * P:(j + 1) * P], q[:, j * P:L], start=True, stop=True)
                    else:
                        for a in range(GROUP):
                            h = GROUP * g + a
                            q, k = Qs[:, h % HALF, h // HALF, :], Ks[:, h % HALF, h // HALF, :]
                            at = a * 256
                            ins = pe.matmul(psum[:, lo + at // BANK, at % BANK:at % BANK + 256],
                                            k[:, 2 * P:3 * P], q[:, 2 * P:L], start=True, stop=True)
                    ins.then_inc(scores_ready, 1)

            def values(b, g):
                if absent(b):
                    return
                pe.wait_ge(masked, count(masked, b, 3 * g + 3))
                if g == 0:
                    pe.wait_ge(v_ready, count(v_ready, b, 2))
                if due(c := count(oT_ready, b, g)):
                    pe.wait_ge(oT_ready, c)
                for j in range(T):
                    for a in range(GROUP):
                        at = a * 1024 + TILE_AT[j] if j != 2 else TILE2_AT + a * 256
                        ins = pe.matmul(sum_bank[32 * a:32 * a + 32, j * P:L], V1[:, j, GROUP * g + a, :],
                                        A[:, g % 2, at:at + L - j * P], start=(j == 0), stop=(j == T - 1))
                ins.then_inc(values_summed, 1)

            def o_rows(b, t):
                if absent(b):
                    return
                if t == 0:
                    pe.wait_ge(oT_ready, count(oT_ready, b, GROUPS))
                    if not absent(b + 1):
                        pe.wait_ge(rest_ready, count(rest_ready, b + 1, 4))
                    else:
                        pe.wait_ge(v_ready, count(v_ready, b, 2))
                else:
                    pe.wait_ge(o_normed, count(o_normed, b, t))
                for g in range(GROUPS):
                    ins = pe.transpose(att_bank[:, g * P:(g + 1) * P], oT[:, g, t * P:(t + 1) * P], ident[:, :])
                ins.then_inc(o_in_psum, 1)

            def onT_transpose(b, k):
                if absent(b):
                    return
                if k == 0:
                    pe.wait_ge(o_normed, count(o_normed, b, T))
                else:
                    pe.wait_ge(onT_ready, count(onT_ready, b, k))
                transpose_rows(att_bank, tok, k).then_inc(onT_in_psum, 1)

            def wo_product(b, j):
                if absent(b):
                    return
                if j == 0:
                    pe.wait_ge(onT_ready, count(onT_ready, b, KD))
                else:
                    pe.wait_ge(x1_ready, count(x1_ready, b, j))
                token_product(att_bank, j, onT, wo, KD).then_inc(wo_in_psum, 1)

            def norm2_transpose(b, k):
                if absent(b):
                    return
                if k == 0:
                    pe.wait_ge(xn2_ready, count(xn2_ready, b, 1))
                else:
                    pe.wait_ge(xn2T_ready, count(xn2T_ready, b, k))
                transpose_rows(mix_bank, xn2, k).then_inc(xn2T_in_psum, 1)

            def context_up(b, f):
                if absent(b):
                    return
                if f == 0:
                    pe.wait_ge(ctx_loaded, count(ctx_loaded, b, 32))
                    pe.wait_ge(xn2T_ready, count(xn2T_ready, b, KD))
                else:
                    pe.wait_ge(gated, count(gated, b, f))
                product(mix_bank, [(ctxT[:, k, f * P:(f + 1) * P], xn2T[:, k, :]) for k in range(KD)])\
                    .then_inc(h1_in_psum, 1)

            def context_down(b, j):
                if absent(b):
                    return
                if j == 0:
                    pe.wait_ge(gated, count(gated, b, T))
                else:
                    pe.wait_ge(x2_ready, count(x2_ready, b, j))
                token_product(mix_bank, j, gT, ctxR, T).then_inc(mix_in_psum, 1)

            def xqT_transpose(b):
                if absent(b):
                    return
                pe.wait_ge(xq_ready, count(xq_ready, b, 1))
                wide = ffn_bank.bitcast(bf16)
                for k in range(KD):
                    for t in range(T):
                        ins = pe.transpose(wide[:, k * L + t * P:k * L + (t + 1) * P],
                                           xq[:, t, k * P:(k + 1) * P], identb[:, :])
                ins.then_inc(xqT_in_psum, 1)

            def spread_scales(s):
                for t in range(T):
                    ins = pe.transpose(ffn_bank[:, t * P:(t + 1) * P], s[:, t:t + 1].to_broadcast([P, P]), ident[:, :])
                return ins

            def spread_token_scales(b):
                if absent(b):
                    return
                pe.wait_ge(xqT_ready, count(xqT_ready, b, 1))
                spread_scales(sdq).then_inc(s_in_psum, 1)

            def ffn_up(b, f):
                if absent(b):
                    return
                if f == 0:
                    pe.wait_ge(xqT_ready, count(xqT_ready, b, 1))
                    pe.wait_ge(sB_ready, count(sB_ready, b, 1))
                else:
                    pe.wait_ge(hs_ready, count(hs_ready, b, f))
                product(ffn_bank, [(w_up_q[:, k, f * P:(f + 1) * P], xqT[:, k, :]) for k in range(KD)])\
                    .then_inc(up_in_psum, 1)

            def hidden_max_rows(b):
                if absent(b):
                    return
                pe.wait_ge(am_ready, count(am_ready, b, 2))
                for t in range(T):
                    ins = pe.transpose(ffn_bank[:, t * P:(t + 1) * P], am[:, t * P:(t + 1) * P], ident[:, :])
                ins.then_inc(amT_in_psum, 1)

            def spread_hidden_scales(b):
                if absent(b):
                    return
                pe.wait_ge(s2_ready, count(s2_ready, b, 1))
                spread_scales(sc4).then_inc(s2_in_psum, 1)

            def ffn_down(b, j):
                if absent(b):
                    return
                if j == 0:
                    pe.wait_ge(s2B_ready, count(s2B_ready, b, 1))
                    pe.wait_ge(hq_ready, count(hq_ready, b, NF // 2))
                else:
                    pe.wait_ge(out_ready, count(out_ready, b, j))
                token_product(ffn_bank, j, hq, w_dn_q, NF).then_inc(down_in_psum, 1)

            def weights_total():
                pe.wait_ge(wsum_ready, 1)
                pe.matmul(ffn_bank[:, 0:2], ones[:, :], wsum[:, :], start=True, stop=True).then_inc(wtotal_ready, 1)

            def iteration(i, second=False):
                ffn_up(i - 3, 6)
                scores(i - 1, 6, 7)
                norm2_transpose(i - 2, 0)
                ffn_up(i - 3, 7)
                scores(i - 1, 8)
                norm2_transpose(i - 2, 1)
                scores(i - 1, 9)
                context_up(i - 2, 0)
                values(i - 1, 0)
                if second:
                    weights_total()
                scores(i - 1, 10, 11)
                norm1_transpose(i, 0)
                values(i - 1, 1)
                norm1_transpose(i, 1)
                scores(i - 1, 12, 13)
                hidden_max_rows(i - 3)
                context_up(i - 2, 1)
                spread_hidden_scales(i - 3)
                qk(i, 0)
                context_up(i - 2, 2)
                scores(i - 1, 14, 15)
                qk(i, 1)
                scores(i - 1, 16)
                ffn_down(i - 3, 0)
                context_up(i - 2, 3)
                ffn_down(i - 3, 1)
                context_down(i - 2, 0)
                scores(i - 1, 17, 18)
                context_down(i - 2, 1)
                qk(i, 2)
                scores(i - 1, 19)
                values(i - 1, 2)
                qk(i, 3)
                values(i - 1, 3)
                o_rows(i - 1, 0)
                xqT_transpose(i - 2)
                o_rows(i - 1, 1)
                spread_token_scales(i - 2)
                o_rows(i - 1, 2)
                ffn_up(i - 2, 0)
                o_rows(i - 1, 3)
                ffn_up(i - 2, 1)
                onT_transpose(i - 1, 0)
                ffn_up(i - 2, 2)
                onT_transpose(i - 1, 1)
                wo_product(i - 1, 0)
                ffn_up(i - 2, 3)
                scores(i, 0)
                wo_product(i - 1, 1)
                ffn_up(i - 2, 4)
                scores(i, 1, 2, 3)
                ffn_up(i - 2, 5)
                v(i, 0)
                scores(i, 4, 5)
                v(i, 1)

            pe.wait_ge(consts_ready, 9)
            pe.wait_ge(w_qkv_loaded, 16 * 2)
            iteration(0)
            pe.wait_ge(w_rest_loaded, 16 * 3)
            iteration(1, second=True)
            pe.wait_ge(weights_quantised, 2)
            iteration(2)
            with pe.Fori(3, B) as i:
                iteration(i)
            for i in range(B, B + 3):
                iteration(i)


def kernel(**inputs):
    import numpy as np
    import concourse.bacc as bacc
    from concourse.bass_utils import run_bass_kernel_spmd

    a = {n: np.asarray(v) for n, v in inputs.items()}
    D = a["x"].shape[2]
    H = 16
    P = 128

    def dims_outside_heads(w):
        return w.reshape(D, 2, H // 2, D // H).transpose(0, 1, 3, 2).reshape(D, D)

    conv_w = a["L0_ffn_conv_w"]
    arrays = {
        "x": a["x"],
        "ctx_rows": a["ctx_1024"],
        "ctx_cols": a["ctx_1024"].transpose(0, 2, 1),
        "w_qk": np.concatenate([dims_outside_heads(a["L0_attn_Wq"]), dims_outside_heads(a["L0_attn_Wk"])], axis=1),
        "w_v": a["L0_attn_Wv"],
        "w_o": a["L0_attn_Wo"],
        "w_up": a["L0_ffn_w1"].T,
        "conv_w": conv_w.reshape(-1, P, 3).transpose(1, 0, 2),
        "conv_b": a["L0_ffn_conv_b"].reshape(-1, P).T,
        "w_down": a["L0_ffn_w2"].T,
    }
    arrays = {n: np.ascontiguousarray(v) for n, v in arrays.items()}
    nc = bacc.Bacc("TRN2", target_bir_lowering=False, num_devices=1, dynamic_dma_scratch_size=1024)
    args = [nc.dram_tensor(n, v.shape, mybir.dt.from_np(v.dtype), kind="ExternalInput").ap()
            for n, v in arrays.items()]
    out = nc.dram_tensor("out", a["x"].shape, mybir.dt.from_np(a["x"].dtype), kind="ExternalOutput").ap()
    decoder_layer(nc, *args, out)
    return run_bass_kernel_spmd(nc, [arrays], core_ids=[0]).results[0]["out"]
```

```python
import concourse.bass as bass
from concourse import mybir
from contextlib import ExitStack


def decoder_layer(nc, x, ctx_rows, ctx_cols, w_qk, w_v, w_o, w_up, conv_w, conv_b, w_down, out):
    fp32 = mybir.dt.float32
    bf16 = mybir.dt.bfloat16
    ALU = mybir.AluOpType
    ACT = mybir.ActivationFunctionType
    AX = mybir.AxisListType

    B, L, D = x.shape
    F = w_up.shape[1]
    P = 128
    T = L // P
    KD = D // P
    NF = F // P
    HEADS, HD = 16, 16
    GROUP = 4
    GROUPS = HEADS // GROUP
    HALF = HEADS // 2
    BANK = 512
    QSCALE = float(HD) ** -0.5
    LN_EPS = 1e-5
    DEN_EPS = 1e-5
    CLIP = 1e-5
    MAGIC = 12582912.0
    PIECES = GROUP + 1
    NP = GROUPS * PIECES
    TILE_AT = [0, 640, None, 512]
    TILE2_AT = GROUP * 1024

    Q_PART = [0, 0, 1, 1, 0, 2, 1, 2]
    K_PART = [0, 1, 0, 1, 2, 0, 2, 1]
    NG = len(Q_PART)

    with ExitStack() as stack:
        def sb(name, shape, dt=fp32):
            return stack.enter_context(nc.sbuf_tensor(name, shape, dt))

        def sem(name):
            return stack.enter_context(nc.semaphore(name))

        ident = sb("ident", [P, P])
        identb = sb("identb", [P, P], bf16)
        ones = sb("ones", [P, P])
        neg_half = sb("neg_half", [P, T])
        wqk = sb("wqk", [P, KD, 2 * D])
        wv = sb("wv", [P, KD, D])
        wo = sb("wo", [P, KD, D])
        w_up_q = sb("w_up_q", [P, KD, F], bf16)
        w_dn_q = sb("w_dn_q", [P, NF, D], bf16)
        cw = sb("cw", [P, NF, 3])
        cb = sb("cb", [P, NF])
        wsum = sb("wsum", [P, 2])
        wmean = sb("wmean", [P, 2])
        wscale = sb("wscale", [P, 2])
        wundo = sb("wundo", [P, 2])

        x_in = sb("x_in", [P, T, D])
        tok = sb("tok", [P, T, D])
        norm1T = sb("norm1T", [P, KD, L])
        parts = [sb(f"part_{n}", [P, 4, L], bf16) for n in ("high", "mid", "low")]
        rest = sb("rest", [P, 2, L])
        Qs = sb("Qs", [P, HALF, 2, L], bf16)
        Ks = sb("Ks", [P, HALF, 2, L], bf16)
        V1 = sb("V1", [P, T, HEADS, 32])
        st1, mv1, ve1, rs1 = sb("st1", [P, T, 6]), sb("mv1", [P, T, 2]), sb("ve1", [P, T]), sb("rs1", [P, T])

        x_res = sb("x_res", [P, T, D])
        A = sb("A", [P, 2, GROUP * 1280])
        oT = sb("oT", [P, GROUPS, L])
        den = sb("den", [P, T, HEADS])
        rden = sb("rden", [P, T, HEADS])
        onT = sb("onT", [P, KD, L])
        x1 = sb("x1", [P, T, D])

        xn2 = sb("xn2", [P, T, D])
        xn2T = sb("xn2T", [P, KD, L])
        ctxT = sb("ctxT", [P, KD, L])
        ctxR = sb("ctxR", [P, T, D])
        gl = sb("gl", [P, 2, L])
        gT = sb("gT", [P, T, L])
        x2 = sb("x2", [P, T, D])
        st2, mv2, ve2, rs2 = sb("st2", [P, T, 6]), sb("mv2", [P, T, 2]), sb("ve2", [P, T]), sb("rs2", [P, T])

        xn3 = sb("xn3", [P, T, D])
        xq = sb("xq", [P, T, D], bf16)
        xqT = sb("xqT", [P, KD, L], bf16)
        sB = sb("sB", [P, L])
        hs = sb("hs", [P, 2, L + 2])
        cv = sb("cv", [P, 2, L])
        act_out = sb("act_out", [P, NF, L])
        w_raw = act_out[:, :, :].rearrange("p f t -> p (f t)")
        am = sb("am", [P, L])
        s2B = sB
        hq = sb("hq", [P, NF, L], bf16)
        st3, mv3, ve3, rs3 = sb("st3", [P, T, 6]), sb("mv3", [P, T, 2]), sb("ve3", [P, T]), sb("rs3", [P, T])
        mx3, sc3, sdq = sb("mx3", [P, T]), sb("sc3", [P, T]), sb("sdq", [P, T])
        mx4, sc4, sdq4 = sb("mx4", [P, T]), sb("sc4", [P, T]), sb("sdq4", [P, T])

        psum = stack.enter_context(nc.psum_tensor("psum", [P, 8, BANK], fp32))
        XN1T_BANK = (4, 6)
        QK_BANK = (4, 6, 7, 4)
        V_BANK = (4, 7)
        SUM_BANK = (6, 4, 6, 5)
        O_BANK = (7, 6, 5, 7)
        ONT_BANK = (7, 6)
        WO_BANK = (7, 6)
        XN2T_BANK = (7, 4)
        UPCTX_BANK = (7, 5, 6, 5)
        DOWNCTX_BANK = (7, 4)
        UP_BANK = (4, 6, 4, 5, 4, 6, 5, 4)
        DOWN_BANK = (4, 5)
        XQT_BANK = 4
        SCALE_BANK = 6
        MAX_BANK = 7
        HSCALE_BANK = 7

        per = {}

        def psem(name, n):
            per[name] = n
            return sem(name)

        w_qkv_loaded = sem("w_qkv_loaded")
        w_rest_loaded = sem("w_rest_loaded")
        waited = sem("waited")
        raw_loaded = sem("raw_loaded")
        consts_ready = sem("consts_ready")
        setup_dve = sem("setup_dve")
        wsum_ready = sem("wsum_ready")
        wtotal_ready = sem("wtotal_ready")
        weights_quantised = sem("weights_quantised")

        x_in_loaded = psem("x_in_loaded", 16)
        var1_ready = psem("var1_ready", 1)
        rstd1_ready = psem("rstd1_ready", 1)
        xn1_ready = psem("xn1_ready", 1)
        xn1T_in_psum = psem("xn1T_in_psum", KD)
        xn1T_ready = psem("xn1T_ready", KD)
        qk_in_psum = psem("qk_in_psum", 4)
        high_ready = psem("high_ready", 4)
        rest_ready = psem("rest_ready", 4)
        mid_ready = psem("mid_ready", 2)
        low_ready = psem("low_ready", 2)
        q_spread = psem("q_spread", NG * 16)
        k_spread = psem("k_spread", NG * 16)
        v_in_psum = psem("v_in_psum", 2)
        v_ready = psem("v_ready", 2)
        norm1_chain = psem("norm1_chain", 2)

        x_res_ready = psem("x_res_ready", 16)
        scores_ready = psem("scores_ready", NP)
        squared = psem("squared", NP)
        masked = psem("masked", 3 * GROUPS)
        values_summed = psem("values_summed", GROUPS)
        oT_ready = psem("oT_ready", GROUPS)
        o_in_psum = psem("o_in_psum", T)
        o_normed = psem("o_normed", T)
        onT_in_psum = psem("onT_in_psum", KD)
        onT_ready = psem("onT_ready", KD)
        wo_in_psum = psem("wo_in_psum", 2)
        x1_ready = psem("x1_ready", 2)
        den_ready = psem("den_ready", T)
        rden_ready = psem("rden_ready", T)

        ctx_loaded = psem("ctx_loaded", 32)
        var2_ready = psem("var2_ready", 1)
        rstd2_ready = psem("rstd2_ready", 1)
        xn2_ready = psem("xn2_ready", 1)
        xn2T_in_psum = psem("xn2T_in_psum", KD)
        xn2T_ready = psem("xn2T_ready", KD)
        h1_in_psum = psem("h1_in_psum", T)
        gelu_ready = psem("gelu_ready", T)
        gated = psem("gated", T)
        mix_in_psum = psem("mix_in_psum", 2)
        x2_ready = psem("x2_ready", 2)
        norm2_chain = psem("norm2_chain", 2)

        var3_ready = psem("var3_ready", 1)
        rstd3_ready = psem("rstd3_ready", 1)
        xq_ready = psem("xq_ready", 1)
        xqT_in_psum = psem("xqT_in_psum", 1)
        xqT_ready = psem("xqT_ready", 1)
        s_in_psum = psem("s_in_psum", 1)
        sB_ready = psem("sB_ready", 1)
        up_in_psum = psem("up_in_psum", NF)
        hs_ready = psem("hs_ready", NF)
        centre_ready = psem("centre_ready", NF)
        conv_ready = psem("conv_ready", NF)
        silu_ready = psem("silu_ready", NF)
        am_ready = psem("am_ready", 2)
        amT_in_psum = psem("amT_in_psum", 1)
        s2_ready = psem("s2_ready", 1)
        s2_in_psum = psem("s2_in_psum", 1)
        s2B_ready = psem("s2B_ready", 1)
        scaled_on_pool = psem("scaled_on_pool", NF // 2)
        scaled_on_dve = psem("scaled_on_dve", NF // 2)
        hq_ready = psem("hq_ready", NF // 2)
        down_in_psum = psem("down_in_psum", 2)
        out_ready = psem("out_ready", 2)
        rows_stored = psem("rows_stored", 16)
        norm3_chain = psem("norm3_chain", 2)
        quantise_chain = psem("quantise_chain", 6)
        left_ready = psem("left_ready", NF)
        hidden_chain = psem("hidden_chain", 3)

        def count(s, b, n):
            return per[s.name] * b + n

        def due(value):
            return not isinstance(value, int) or value > 0

        def absent(b):
            return isinstance(b, int) and not 0 <= b < B

        def latest(*readers):
            for s, b, n in readers:
                if not absent(b):
                    return s, count(s, b, n)
            return None

        def settle(eng):
            eng.sem_inc(waited, 1)

        class Chain:

            def __init__(self, eng, sem, b, n=0):
                self.eng, self.sem, self.b, self.n = eng, sem, b, n

            def link(self, ins):
                self.n += 1
                ins.then_inc(self.sem, 1)
                self.eng.wait_ge(self.sem, count(self.sem, self.b, self.n))

        def rows(dram, b):
            return dram[bass.ds(b, 1), :, :].rearrange("o (t p) d -> p (o t) d", p=P)

        DEPTH = 3
        LEAD = 3

        block = stack.enter_context(nc.Block())

        @block.sync
        def _(sp):
            def load_x(b):
                if absent(b):
                    return
                if due(c := count(xn1_ready, b, 0)):
                    sp.wait_ge(xn1_ready, c)
                settle(sp)
                if due(c := count(x_res_ready, b, 0)):
                    sp.wait_ge(x_res_ready, c)
                settle(sp)
                sp.dma_start(x_in[:, :, :], rows(x, b)).then_inc(x_in_loaded, 16)

            def copy_x(b):
                if absent(b):
                    return
                sp.wait_ge(x_in_loaded, count(x_in_loaded, b, 16))
                settle(sp)
                if due(c := count(x1_ready, b, 0)):
                    sp.wait_ge(x1_ready, c)
                sp.dma_start(x_res[:, :, :], x_in[:, :, :]).then_inc(x_res_ready, 16)

            def load_ctx(b):
                if absent(b):
                    return
                if due(c := count(mix_in_psum, b, 0)):
                    sp.wait_ge(mix_in_psum, c)
                settle(sp)
                sp.dma_start(ctxT[:, :, :], ctx_cols[bass.ds(b, 1), :, :].rearrange(
                    "o (k p) t -> p (o k) t", p=P)).then_inc(ctx_loaded, 16)
                sp.dma_start(ctxR[:, :, :], rows(ctx_rows, b)).then_inc(ctx_loaded, 16)

            def spread_side(b, side):
                if absent(b):
                    return
                dst, which, spread = ((Qs, Q_PART, q_spread), (Ks, K_PART, k_spread))[side]
                if due(c := count(scores_ready, b, 0)):
                    sp.wait_ge(scores_ready, c)
                settle(sp)
                for part, ready, n in ((0, high_ready, 2), (1, mid_ready, 1), (2, low_ready, 1)):
                    sp.wait_ge(ready, count(ready, b, n * (side + 1)))
                    for g in range(NG):
                        if which[g] == part:
                            sp.dma_start(dst[16 * g:16 * g + 16, :, :, :].rearrange("d h m t -> d (h m t)"),
                                         parts[part][:, 2 * side:2 * side + 2, :].rearrange("p m t -> p (m t)")
                                         ).then_inc(spread, 16)

            def store(b):
                if absent(b):
                    return
                sp.wait_ge(out_ready, count(out_ready, b, 2))
                settle(sp)
                sp.dma_start(rows(out, b), xn3[:, :, :]).then_inc(rows_stored, 16)

            def load_weights():
                sp.dma_start(wqk[:, :, :], w_qk.rearrange("(k p) n -> p k n", p=P)).then_inc(w_qkv_loaded, 16)
                sp.dma_start(wv[:, :, :], w_v.rearrange("(k p) n -> p k n", p=P)).then_inc(w_qkv_loaded, 16)
                sp.dma_start(w_raw[:, 0:KD * F].rearrange("p (k n) -> p k n", k=KD),
                             w_up.rearrange("(k p) n -> p k n", p=P)).then_inc(raw_loaded, 16)
                sp.dma_start(w_raw[:, KD * F:2 * KD * F].rearrange("p (f n) -> p f n", f=NF),
                             w_down.rearrange("(f p) n -> p f n", p=P)).then_inc(raw_loaded, 16)
                sp.dma_start(wo[:, :, :], w_o.rearrange("(k p) n -> p k n", p=P)).then_inc(w_rest_loaded, 16)
                sp.dma_start(cw[:, :, :], conv_w).then_inc(w_rest_loaded, 16)
                sp.dma_start(cb[:, :], conv_b).then_inc(w_rest_loaded, 16)

            def iteration(i, first=False):
                load_ctx(i - 2)
                copy_x(i - 1)
                load_x(i)
                if first:
                    load_weights()
                store(i - 3)
                spread_side(i, 0)
                spread_side(i, 1)

            for i in range(LEAD):
                iteration(i, first=(i == 0))
            with sp.Fori(LEAD, B) as i:
                iteration(i)
            for i in range(B, B + DEPTH):
                iteration(i)
            sp.wait_ge(rows_stored, 16 * B)

        @block.gpsimd
        def _(pool):
            def rstd(b, var_ready, ve, rs, ready):
                if absent(b):
                    return
                pool.wait_ge(var_ready, count(var_ready, b, 1))
                pool.tensor_tensor(rs[:, :], ve[:, :], neg_half[:, :], ALU.pow).then_inc(ready, 1)

            def rstd1(b):
                rstd(b, var1_ready, ve1, rs1, rstd1_ready)

            def rstd2(b):
                rstd(b, var2_ready, ve2, rs2, rstd2_ready)

            def rstd3(b):
                rstd(b, var3_ready, ve3, rs3, rstd3_ready)

            def mask_first(b, g):
                if absent(b):
                    return
                pool.wait_ge(squared, count(squared, b, PIECES * g + GROUP))
                settle(pool)
                first = A[:, g % 2, 0:TILE2_AT].rearrange("p (h n) -> p h n", h=GROUP)[:, :, 0:P]
                pool.affine_select(out=first, in_=first, compare_op=ALU.is_ge, fill=0.0, base=0,
                                   pattern=[[0, GROUP], [1, P]], channel_multiplier=-1).then_inc(masked, 1)

            def mask_pair(b, g):
                if absent(b):
                    return
                pair = A[:, g % 2, 0:TILE2_AT].rearrange("p (h n) -> p h n", h=GROUP)[
                    :, :, TILE_AT[3]:TILE_AT[3] + 2 * P].rearrange("p h (j c) -> p h j c", j=2)
                pool.affine_select(out=pair, in_=pair, compare_op=ALU.is_ge, fill=0.0, base=0,
                                   pattern=[[0, GROUP], [0, 2], [1, P]], channel_multiplier=-1).then_inc(masked, 1)

            def mask_last(b, g):
                if absent(b):
                    return
                pool.wait_ge(squared, count(squared, b, PIECES * g + PIECES))
                settle(pool)
                second = A[:, g % 2, TILE2_AT:TILE2_AT + 1024].rearrange("p (h n) -> p h n", h=GROUP)[:, :, 0:P]
                pool.affine_select(out=second, in_=second, compare_op=ALU.is_ge, fill=0.0, base=0,
                                   pattern=[[0, GROUP], [1, P]], channel_multiplier=-1).then_inc(masked, 1)

            def low_part(b, side):
                if absent(b):
                    return
                pool.wait_ge(rest_ready, count(rest_ready, b, 2 * side + 2))
                pool.wait_ge(mid_ready, count(mid_ready, b, side + 1))
                pool.tensor_tensor(parts[2][:, 2 * side:2 * side + 2, :], rest[:, :, :],
                                   parts[1][:, 2 * side:2 * side + 2, :], ALU.subtract).then_inc(low_ready, 1)

            def scale_hidden(b, f):
                if absent(b):
                    return
                pool.wait_ge(s2B_ready, count(s2B_ready, b, 1))
                pool.tensor_tensor(act_out[:, f, :], act_out[:, f, :], s2B[:, :], ALU.mult).then_inc(scaled_on_pool, 1)

            def iteration(i):
                mask_pair(i - 1, 0)
                mask_last(i - 1, 0)
                rstd1(i)
                mask_first(i - 1, 1)
                mask_pair(i - 1, 1)
                mask_last(i - 1, 1)
                mask_first(i - 1, 2)
                scale_hidden(i - 3, 0)
                scale_hidden(i - 3, 1)
                scale_hidden(i - 3, 2)
                scale_hidden(i - 3, 3)
                mask_pair(i - 1, 2)
                low_part(i, 0)
                mask_last(i - 1, 2)
                rstd3(i - 2)
                mask_first(i - 1, 3)
                mask_pair(i - 1, 3)
                mask_last(i - 1, 3)
                low_part(i, 1)
                rstd2(i - 1)
                mask_first(i, 0)

            pool.memset(ident[:, :], 0.0).then_inc(consts_ready, 1)
            pool.memset(ones[:, :], 1.0).then_inc(consts_ready, 1)
            pool.memset(neg_half[:, :], -0.5).then_inc(consts_ready, 1)
            pool.wait_ge(consts_ready, 3)
            pool.affine_select(out=ident[:, :], in_=ident[:, :], compare_op=ALU.not_equal, fill=1.0,
                               base=0, pattern=[[-1, P]], channel_multiplier=1).then_inc(consts_ready, 1)
            pool.memset(V1[:, :, :, HD:32], 0.0).then_inc(consts_ready, 1)
            pool.wait_ge(consts_ready, 5)
            pool.memset(V1[:, :, :, HD:HD + 1], 1.0).then_inc(consts_ready, 1)
            pool.memset(hs[:, :, 0:1], 0.0).then_inc(consts_ready, 1)
            pool.memset(hs[:, :, L + 1:L + 2], 0.0).then_inc(consts_ready, 1)
            for i in range(LEAD):
                iteration(i)
            with pool.Fori(LEAD, B) as i:
                iteration(i)
            for i in range(B, B + DEPTH):
                iteration(i)

        @block.scalar
        def _(act):
            def xn1T_copy(b, k):
                if absent(b):
                    return
                act.wait_ge(xn1T_in_psum, count(xn1T_in_psum, b, k + 1))
                if k == 0:
                    if due(c := count(v_in_psum, b, 0)):
                        act.wait_ge(v_in_psum, c)
                act.activation(norm1T[:, k, :], psum[:, XN1T_BANK[k], :], ACT.Copy).then_inc(xn1T_ready, 1)

            def high_part(b, m):
                if absent(b):
                    return
                act.wait_ge(qk_in_psum, count(qk_in_psum, b, m + 1))
                if m == 0:
                    if due(c := count(q_spread, b, 0)):
                        act.wait_ge(q_spread, c)
                if m == 2:
                    if due(c := count(k_spread, b, 0)):
                        act.wait_ge(k_spread, c)
                act.activation(parts[0][:, m, :], psum[:, QK_BANK[m], :], ACT.Copy).then_inc(high_ready, 1)

            def v_copy(b, j):
                if absent(b):
                    return
                act.wait_ge(v_in_psum, count(v_in_psum, b, j + 1))
                if j == 0:
                    if due(c := count(values_summed, b, 0)):
                        act.wait_ge(values_summed, c)
                act.activation(V1[:, 2 * j:2 * j + 2, :, 0:HD],
                               psum[:, V_BANK[j], :].rearrange("p (t h d) -> p t h d", t=2, h=HEADS),
                               ACT.Copy).then_inc(v_ready, 1)

            def square(b, *pieces):
                if absent(b):
                    return
                for p in pieces:
                    g, n = p // PIECES, p % PIECES
                    act.wait_ge(scores_ready, count(scores_ready, b, p + 1))
                    if n == 0:
                        if due(c := count(values_summed, b, g - 1)):
                            act.wait_ge(values_summed, c)
                    act.activation(A[:, g % 2, n * 1024:(n + 1) * 1024],
                                   psum[:, 2 * (p % 2):2 * (p % 2) + 2, :].rearrange("p a n -> p (a n)"),
                                   ACT.Square, scale=QSCALE).then_inc(squared, 1)

            def oT_copy(b, g):
                if absent(b):
                    return
                act.wait_ge(values_summed, count(values_summed, b, g + 1))
                if g == 0:
                    if due(c := count(o_in_psum, b, 0)):
                        act.wait_ge(o_in_psum, c)
                act.activation(oT[:, g, :], psum[:, SUM_BANK[g], :], ACT.Copy).then_inc(oT_ready, 1)

            def onT_copy(b, k):
                if absent(b):
                    return
                act.wait_ge(onT_in_psum, count(onT_in_psum, b, k + 1))
                if k == 0:
                    if due(c := count(wo_in_psum, b, 0)):
                        act.wait_ge(wo_in_psum, c)
                act.activation(onT[:, k, :], psum[:, ONT_BANK[k], :], ACT.Copy).then_inc(onT_ready, 1)

            def xn2T_copy(b, k):
                if absent(b):
                    return
                act.wait_ge(xn2T_in_psum, count(xn2T_in_psum, b, k + 1))
                act.activation(xn2T[:, k, :], psum[:, XN2T_BANK[k], :], ACT.Copy).then_inc(xn2T_ready, 1)

            def gelu(b, f):
                if absent(b):
                    return
                act.wait_ge(h1_in_psum, count(h1_in_psum, b, f + 1))
                if due(c := count(gated, b, f - 1)):
                    act.wait_ge(gated, c)
                act.activation(gl[:, f % 2, :], psum[:, UPCTX_BANK[f], :], ACT.Gelu).then_inc(gelu_ready, 1)

            def xqT_copy(b):
                if absent(b):
                    return
                act.wait_ge(xqT_in_psum, count(xqT_in_psum, b, 1))
                act.activation(xqT[:, :, :].rearrange("p k t -> p (k t)"), psum[:, XQT_BANK, :].bitcast(bf16), ACT.Copy)\
                    .then_inc(xqT_ready, 1)

            def sB_copy(b):
                if absent(b):
                    return
                act.wait_ge(s_in_psum, count(s_in_psum, b, 1))
                act.activation(sB[:, :], psum[:, SCALE_BANK, :], ACT.Copy).then_inc(sB_ready, 1)

            def centre_tap(b, f):
                if absent(b):
                    return
                act.wait_ge(hs_ready, count(hs_ready, b, f + 1))
                if f >= 2:
                    act.wait_ge(silu_ready, count(silu_ready, b, f - 1))
                act.activation(cv[:, f % 2, :], hs[:, f % 2, 1:L + 1], ACT.Identity,
                               scale=cw[:, f, 1:2], bias=cb[:, f:f + 1]).then_inc(centre_ready, 1)

            def silu(b, f):
                if absent(b):
                    return
                act.wait_ge(conv_ready, count(conv_ready, b, f + 1))
                act.activation(act_out[:, f, :], cv[:, f % 2, :], ACT.Silu).then_inc(silu_ready, 1)

            def s2B_copy(b):
                if absent(b):
                    return
                act.wait_ge(s2_in_psum, count(s2_in_psum, b, 1))
                act.activation(s2B[:, :], psum[:, HSCALE_BANK, :], ACT.Copy).then_inc(s2B_ready, 1)

            def iteration(i):
                centre_tap(i - 3, 6)
                silu(i - 3, 5)
                square(i - 1, 8)
                centre_tap(i - 3, 7)
                square(i - 1, 9)
                oT_copy(i - 1, 0)
                xn1T_copy(i, 0)
                silu(i - 3, 6)
                silu(i - 3, 7)
                xn1T_copy(i, 1)
                square(i - 1, 10, 11)
                oT_copy(i - 1, 1)
                gelu(i - 2, 0)
                gelu(i - 2, 1)
                square(i - 1, 12)
                gelu(i - 2, 2)
                square(i - 1, 13)
                high_part(i, 0)
                s2B_copy(i - 3)
                gelu(i - 2, 3)
                square(i - 1, 14, 15)
                high_part(i, 1)
                square(i - 1, 16, 17)
                high_part(i, 2)
                square(i - 1, 18, 19)
                high_part(i, 3)
                oT_copy(i - 1, 2)
                oT_copy(i - 1, 3)
                sB_copy(i - 2)
                xqT_copy(i - 2)
                centre_tap(i - 2, 0)
                centre_tap(i - 2, 1)
                v_copy(i, 0)
                onT_copy(i - 1, 0)
                onT_copy(i - 1, 1)
                silu(i - 2, 0)
                silu(i - 2, 1)
                centre_tap(i - 2, 2)
                square(i, 0, 1)
                centre_tap(i - 2, 3)
                silu(i - 2, 2)
                square(i, 2, 3)
                v_copy(i, 1)
                square(i, 4, 5)
                centre_tap(i - 2, 4)
                silu(i - 2, 3)
                xn2T_copy(i - 1, 0)
                centre_tap(i - 2, 5)
                xn2T_copy(i - 1, 1)
                silu(i - 2, 4)
                square(i, 6, 7)

            for i in range(LEAD):
                iteration(i)
            with act.Fori(LEAD, B) as i:
                iteration(i)
            for i in range(B, B + DEPTH):
                iteration(i)

        @block.vector
        def _(dve):
            def norm_stats(chain, src, st, t0=0):
                for t in range(t0, T):
                    ins = dve.bn_stats(st[:, t, :], src[:, t, :])
                ins.then_inc(chain, 1)

            def norm_aggregate(chain, b, st, mv):
                if absent(b):
                    return
                dve.wait_ge(chain, count(chain, b, 1))
                settle(dve)
                for t in range(T):
                    ins = dve.bn_aggr(mv[:, t, :], st[:, t, :])
                ins.then_inc(chain, 1)

            def norm_variance(chain, b, mv, ve, var_ready):
                if absent(b):
                    return
                dve.wait_ge(chain, count(chain, b, 2))
                dve.tensor_scalar(ve[:, :], mv[:, :, 1], LN_EPS, None, ALU.add).then_inc(var_ready, 1)

            def norm_apply(dst, src, mv, rs):
                for t in range(T):
                    ins = dve.tensor_scalar(dst[:, t, :], src[:, t, :], mv[:, t, 0:1], rs[:, t:t + 1],
                                            ALU.subtract, ALU.mult)
                return ins

            def stats1(b):
                if absent(b):
                    return
                dve.wait_ge(x_in_loaded, count(x_in_loaded, b, 16))
                norm_stats(norm1_chain, x_in, st1)

            def aggregate1(b):
                norm_aggregate(norm1_chain, b, st1, mv1)

            def variance1(b):
                norm_variance(norm1_chain, b, mv1, ve1, var1_ready)

            def norm1(b):
                if absent(b):
                    return
                dve.wait_ge(rstd1_ready, count(rstd1_ready, b, 1))
                if due(c := count(onT_in_psum, b, -KD)):
                    dve.wait_ge(onT_in_psum, c)
                norm_apply(tok, x_in, mv1, rs1).then_inc(xn1_ready, 1)

            def rest_part(b, m):
                if absent(b):
                    return
                dve.wait_ge(high_ready, count(high_ready, b, m + 1))
                if due(c := count(low_ready, b, m // 2)):
                    dve.wait_ge(low_ready, c)
                dve.tensor_tensor(rest[:, m % 2, :], psum[:, QK_BANK[m], :], parts[0][:, m, :], ALU.subtract)\
                    .then_inc(rest_ready, 1)

            def mid_part(b, side):
                if absent(b):
                    return
                dve.wait_ge(rest_ready, count(rest_ready, b, 2 * side + 2))
                dve.tensor_copy(parts[1][:, 2 * side:2 * side + 2, :], rest[:, :, :]).then_inc(mid_ready, 1)

            def denominator(b, t):
                if absent(b):
                    return
                dve.wait_ge(o_in_psum, count(o_in_psum, b, t + 1))
                dve.tensor_scalar(den[:, t, :], psum[:, O_BANK[t], :].rearrange("p (h n) -> p h n", n=32)[:, :, HD],
                                  DEN_EPS, None, ALU.add).then_inc(den_ready, 1)

            def reciprocal(b, t):
                if absent(b):
                    return
                dve.wait_ge(den_ready, count(den_ready, b, t + 1))
                dve.reciprocal(rden[:, t, :], den[:, t, :]).then_inc(rden_ready, 1)

            def divide(b, t):
                if absent(b):
                    return
                dve.wait_ge(rden_ready, count(rden_ready, b, t + 1))
                if t == 0 and not absent(b + 1):
                    dve.wait_ge(xn1T_in_psum, count(xn1T_in_psum, b + 1, KD))
                dve.tensor_tensor(tok[:, t, :].rearrange("p (h d) -> p h d", h=HEADS),
                                  psum[:, O_BANK[t], :].rearrange("p (h n) -> p h n", n=32)[:, :, 0:HD],
                                  rden[:, t, :].unsqueeze(2).to_broadcast([P, HEADS, HD]), ALU.mult)\
                    .then_inc(o_normed, 1)

            def add_attention(b, j):
                if absent(b):
                    return
                if j == 0:
                    dve.wait_ge(x_res_ready, count(x_res_ready, b, 16))
                dve.wait_ge(wo_in_psum, count(wo_in_psum, b, j + 1))
                dve.tensor_tensor(x1[:, 2 * j:2 * j + 2, :].rearrange("p t d -> p (t d)"), psum[:, WO_BANK[j], :],
                                  x_res[:, 2 * j:2 * j + 2, :].rearrange("p t d -> p (t d)"), ALU.add)\
                    .then_inc(x1_ready, 1)

            def stats2_first(b):
                if absent(b):
                    return
                dve.wait_ge(x1_ready, count(x1_ready, b, 1))
                for t in range(T // 2):
                    dve.bn_stats(st2[:, t, :], x1[:, t, :])

            def stats2(b):
                if absent(b):
                    return
                dve.wait_ge(x1_ready, count(x1_ready, b, 2))
                norm_stats(norm2_chain, x1, st2, T // 2)

            def aggregate2(b):
                norm_aggregate(norm2_chain, b, st2, mv2)

            def variance2(b):
                norm_variance(norm2_chain, b, mv2, ve2, var2_ready)

            def norm2(b):
                if absent(b):
                    return
                dve.wait_ge(rstd2_ready, count(rstd2_ready, b, 1))
                norm_apply(xn2, x1, mv2, rs2).then_inc(xn2_ready, 1)

            def gate(b, f):
                if absent(b):
                    return
                dve.wait_ge(gelu_ready, count(gelu_ready, b, f + 1))
                dve.tensor_tensor(gT[:, f, :], psum[:, UPCTX_BANK[f], :], gl[:, f % 2, :], ALU.mult).then_inc(gated, 1)

            def add_mix(b, j):
                if absent(b):
                    return
                if j == 0:
                    if due(c := count(out_ready, b, 0)):
                        dve.wait_ge(out_ready, c)
                dve.wait_ge(mix_in_psum, count(mix_in_psum, b, j + 1))
                dve.tensor_tensor(x2[:, 2 * j:2 * j + 2, :].rearrange("p t d -> p (t d)"), psum[:, DOWNCTX_BANK[j], :],
                                  x1[:, 2 * j:2 * j + 2, :].rearrange("p t d -> p (t d)"), ALU.add)\
                    .then_inc(x2_ready, 1)

            def stats3_first(b):
                if absent(b):
                    return
                dve.wait_ge(x2_ready, count(x2_ready, b, 1))
                for t in range(T // 2):
                    dve.bn_stats(st3[:, t, :], x2[:, t, :])

            def stats3(b):
                if absent(b):
                    return
                dve.wait_ge(x2_ready, count(x2_ready, b, 2))
                norm_stats(norm3_chain, x2, st3, T // 2)

            def aggregate3(b):
                norm_aggregate(norm3_chain, b, st3, mv3)

            def variance3(b):
                norm_variance(norm3_chain, b, mv3, ve3, var3_ready)

            def scales(chain, mx, sc, sd, w):
                chain.link(dve.tensor_scalar(mx[:, :], mx[:, :], CLIP, None, ALU.max))
                chain.link(dve.reciprocal(sc[:, :], mx[:, :]))
                dve.tensor_scalar(sd[:, :], mx[:, :], wundo[:, w:w + 1], None, ALU.mult)
                return dve.tensor_scalar(sc[:, :], sc[:, :], 127.0, None, ALU.mult)

            def norm3(b):
                if absent(b):
                    return
                dve.wait_ge(rstd3_ready, count(rstd3_ready, b, 1))
                if due(c := count(rows_stored, b, 0)):
                    dve.wait_ge(rows_stored, c)
                norm_apply(xn3, x2, mv3, rs3).then_inc(quantise_chain, 1)

            def row_max(b):
                if absent(b):
                    return
                dve.wait_ge(quantise_chain, count(quantise_chain, b, 1))
                dve.tensor_reduce(mx3[:, :], xn3[:, :, :], AX.X, ALU.max, apply_absolute_value=True)\
                    .then_inc(quantise_chain, 1)

            def token_scales(b):
                if absent(b):
                    return
                dve.wait_ge(quantise_chain, count(quantise_chain, b, 2))
                Chain(dve, quantise_chain, b, 4).link(scales(Chain(dve, quantise_chain, b, 2), mx3, sc3, sdq, 0))

            def round_rows(b):
                if absent(b):
                    return
                for t in range(T):
                    ins = dve.tensor_scalar(xn3[:, t, :], xn3[:, t, :], sc3[:, t:t + 1], MAGIC, ALU.mult, ALU.add)
                ins.then_inc(quantise_chain, 1)

            def integer_rows(b):
                if absent(b):
                    return
                dve.wait_ge(quantise_chain, count(quantise_chain, b, 6))
                dve.tensor_scalar(xq[:, :, :], xn3[:, :, :], -MAGIC, None, ALU.add).then_inc(xq_ready, 1)

            def up_scaled(b, f):
                if absent(b):
                    return
                dve.wait_ge(up_in_psum, count(up_in_psum, b, f + 1))
                if f == 0:
                    dve.wait_ge(sB_ready, count(sB_ready, b, 1))
                if f >= 2:
                    dve.wait_ge(conv_ready, count(conv_ready, b, f - 1))
                dve.tensor_tensor(hs[:, f % 2, 1:L + 1], psum[:, UP_BANK[f], :], sB[:, :], ALU.mult).then_inc(hs_ready, 1)

            def left_tap(b, f):
                if absent(b):
                    return
                dve.wait_ge(centre_ready, count(centre_ready, b, f + 1))
                dve.scalar_tensor_tensor(out=cv[:, f % 2, :], in0=hs[:, f % 2, 0:L], scalar=cw[:, f, 0:1],
                                         in1=cv[:, f % 2, :], op0=ALU.mult, op1=ALU.add).then_inc(left_ready, 1)

            def right_tap(b, f):
                if absent(b):
                    return
                dve.wait_ge(left_ready, count(left_ready, b, f + 1))
                dve.scalar_tensor_tensor(out=cv[:, f % 2, :], in0=hs[:, f % 2, 2:L + 2], scalar=cw[:, f, 2:3],
                                         in1=cv[:, f % 2, :], op0=ALU.mult, op1=ALU.add)\
                    .then_inc(conv_ready, 1)

            def hidden_max(b):
                if absent(b):
                    return
                dve.wait_ge(silu_ready, count(silu_ready, b, NF))
                for half in (slice(0, L // 2), slice(L // 2, L)):
                    dve.tensor_reduce(am[:, half], act_out[:, :, half].rearrange("p f t -> p t f"), AX.X, ALU.max,
                                      apply_absolute_value=True).then_inc(am_ready, 1)

            def token_max(b):
                if absent(b):
                    return
                dve.wait_ge(amT_in_psum, count(amT_in_psum, b, 1))
                dve.tensor_reduce(mx4[:, :], psum[:, MAX_BANK, :].rearrange("p (t n) -> p t n", t=T), AX.X, ALU.max)\
                    .then_inc(hidden_chain, 1)

            def hidden_scales(b):
                if absent(b):
                    return
                dve.wait_ge(hidden_chain, count(hidden_chain, b, 1))
                scales(Chain(dve, hidden_chain, b, 1), mx4, sc4, sdq4, 1).then_inc(s2_ready, 1)

            def scale_hidden(b, f):
                if absent(b):
                    return
                dve.wait_ge(s2B_ready, count(s2B_ready, b, 1))
                dve.tensor_tensor(act_out[:, f, :], act_out[:, f, :], s2B[:, :], ALU.mult).then_inc(scaled_on_dve, 1)

            def hidden_round(b, j):
                if absent(b):
                    return
                if j < NF // 4:
                    dve.wait_ge(scaled_on_pool, count(scaled_on_pool, b, 2 * j + 2))
                else:
                    dve.wait_ge(scaled_on_dve, count(scaled_on_dve, b, 2 * j + 2 - NF // 2))
                dve.tensor_scalar(hq[:, 2 * j:2 * j + 2, :], act_out[:, 2 * j:2 * j + 2, :], MAGIC, -MAGIC,
                                  ALU.add, ALU.add).then_inc(hq_ready, 1)

            def finish(b, j):
                if absent(b):
                    return
                if j == 0:
                    dve.wait_ge(s2_ready, count(s2_ready, b, 1))
                dve.wait_ge(down_in_psum, count(down_in_psum, b, j + 1))
                for t in (2 * j, 2 * j + 1):
                    ins = dve.scalar_tensor_tensor(out=xn3[:, t, :], in0=psum[:, DOWN_BANK[j], (t % 2) * D:(t % 2 + 1) * D],
                                                   scalar=sdq4[:, t:t + 1], in1=x2[:, t, :],
                                                   op0=ALU.mult, op1=ALU.add)
                ins.then_inc(out_ready, 1)

            def sum_weights():
                dve.wait_ge(raw_loaded, 32)
                dve.tensor_reduce(wsum[:, 0:1], w_raw[:, 0:KD * F], AX.X, ALU.add, apply_absolute_value=True)
                dve.tensor_reduce(wsum[:, 1:2], w_raw[:, KD * F:2 * KD * F], AX.X, ALU.add,
                                  apply_absolute_value=True).then_inc(wsum_ready, 1)

            def quantise_weights():
                n = [0]

                def link(ins):
                    n[0] += 1
                    ins.then_inc(setup_dve, 1)
                    dve.wait_ge(setup_dve, n[0])

                dve.wait_ge(w_rest_loaded, 16 * 3)
                dve.wait_ge(wtotal_ready, 1)
                link(dve.tensor_scalar(wmean[:, :], psum[:, 0, 0:2], 1.0 / (D * F), CLIP, ALU.mult, ALU.max))
                link(dve.reciprocal(wscale[:, :], wmean[:, :]))
                dve.tensor_scalar(wundo[:, :], wmean[:, :], 1.0 / 127.0, None, ALU.mult)
                for w, q in enumerate((w_up_q[:, :, :].rearrange("p k n -> p (k n)"),
                                       w_dn_q[:, :, :].rearrange("p f n -> p (f n)"))):
                    raw = w_raw[:, w * KD * F:(w + 1) * KD * F]
                    link(dve.tensor_scalar(raw, raw, wscale[:, w:w + 1], MAGIC, ALU.mult, ALU.add))
                    link(dve.tensor_scalar(raw, raw, -MAGIC, 1.0, ALU.add, ALU.min))
                    dve.tensor_scalar(q, raw, -1.0, None, ALU.max).then_inc(weights_quantised, 1)

            def iteration(i, weights=False):
                up_scaled(i - 3, 4)
                norm2(i - 2)
                right_tap(i - 3, 3)
                up_scaled(i - 3, 5)
                left_tap(i - 3, 4)
                right_tap(i - 3, 4)
                stats1(i)
                left_tap(i - 3, 5)
                up_scaled(i - 3, 6)
                aggregate1(i)
                right_tap(i - 3, 5)
                variance1(i)
                up_scaled(i - 3, 7)
                left_tap(i - 3, 6)
                norm1(i)
                right_tap(i - 3, 6)
                left_tap(i - 3, 7)
                right_tap(i - 3, 7)
                hidden_max(i - 3)
                gate(i - 2, 0)
                gate(i - 2, 1)
                token_max(i - 3)
                hidden_scales(i - 3)
                gate(i - 2, 2)
                rest_part(i, 0)
                scale_hidden(i - 3, 4)
                gate(i - 2, 3)
                scale_hidden(i - 3, 5)
                scale_hidden(i - 3, 6)
                scale_hidden(i - 3, 7)
                hidden_round(i - 3, 0)
                hidden_round(i - 3, 3)
                hidden_round(i - 3, 2)
                hidden_round(i - 3, 1)
                rest_part(i, 1)
                finish(i - 3, 0)
                finish(i - 3, 1)
                add_mix(i - 2, 0)
                mid_part(i, 0)
                stats3_first(i - 2)
                add_mix(i - 2, 1)
                stats3(i - 2)
                aggregate3(i - 2)
                variance3(i - 2)
                norm3(i - 2)
                row_max(i - 2)
                rest_part(i, 2)
                token_scales(i - 2)
                round_rows(i - 2)
                rest_part(i, 3)
                integer_rows(i - 2)
                mid_part(i, 1)
                if weights:
                    sum_weights()
                    quantise_weights()
                denominator(i - 1, 0)
                reciprocal(i - 1, 0)
                denominator(i - 1, 1)
                divide(i - 1, 0)
                reciprocal(i - 1, 1)
                denominator(i - 1, 2)
                divide(i - 1, 1)
                up_scaled(i - 2, 0)
                reciprocal(i - 1, 2)
                denominator(i - 1, 3)
                up_scaled(i - 2, 1)
                reciprocal(i - 1, 3)
                divide(i - 1, 2)
                divide(i - 1, 3)
                left_tap(i - 2, 0)
                left_tap(i - 2, 1)
                right_tap(i - 2, 0)
                right_tap(i - 2, 1)
                up_scaled(i - 2, 2)
                up_scaled(i - 2, 3)
                add_attention(i - 1, 0)
                stats2_first(i - 1)
                left_tap(i - 2, 2)
                right_tap(i - 2, 2)
                add_attention(i - 1, 1)
                stats2(i - 1)
                aggregate2(i - 1)
                variance2(i - 1)
                left_tap(i - 2, 3)

            dve.wait_ge(consts_ready, 8)
            dve.tensor_copy(identb[:, :], ident[:, :]).then_inc(consts_ready, 1)
            for i in range(LEAD):
                iteration(i, weights=(i == 0))
            with dve.Fori(LEAD, B) as i:
                iteration(i)
            for i in range(B, B + DEPTH):
                iteration(i)

        @block.tensor
        def _(pe):
            def product(dst, pairs):
                for n, (lhsT, rhs) in enumerate(pairs):
                    ins = pe.matmul(dst, lhsT, rhs, start=(n == 0), stop=(n == len(pairs) - 1))
                return ins

            def transpose_rows(bank, src, k):
                for t in range(T):
                    ins = pe.transpose(bank[:, t * P:(t + 1) * P], src[:, t, k * P:(k + 1) * P], ident[:, :])
                return ins

            def token_product(bank, j, lhs, rhs, n):
                for t in (2 * j, 2 * j + 1):
                    ins = product(bank[:, (t % 2) * D:(t % 2 + 1) * D],
                                  [(lhs[:, k, t * P:(t + 1) * P], rhs[:, k, :]) for k in range(n)])
                return ins

            def norm1_transpose(b, k, left):
                if absent(b):
                    return
                if k == 0:
                    pe.wait_ge(xn1_ready, count(xn1_ready, b, 1))
                if left:
                    pe.wait_ge(left[0], left[1])
                transpose_rows(psum[:, XN1T_BANK[k], :], tok, k).then_inc(xn1T_in_psum, 1)

            def qk(b, m, left):
                if absent(b):
                    return
                if m == 0:
                    pe.wait_ge(xn1T_ready, count(xn1T_ready, b, KD))
                if left:
                    pe.wait_ge(left[0], left[1])
                product(psum[:, QK_BANK[m], :], [(wqk[:, k, m * P:(m + 1) * P], norm1T[:, k, :]) for k in range(KD)])\
                    .then_inc(qk_in_psum, 1)

            def v(b, j, left):
                if absent(b):
                    return
                if j == 0:
                    pe.wait_ge(xn1T_ready, count(xn1T_ready, b, KD))
                if left:
                    pe.wait_ge(left[0], left[1])
                token_product(psum[:, V_BANK[j], :], j, norm1T, wv, KD).then_inc(v_in_psum, 1)

            def scores(b, *pieces):
                if absent(b):
                    return
                for p in pieces:
                    g, n = p // PIECES, p % PIECES
                    if p == 0:
                        pe.wait_ge(q_spread, count(q_spread, b, per["q_spread"]))
                        pe.wait_ge(k_spread, count(k_spread, b, per["k_spread"]))
                    if due(c := count(squared, b, p - 1)):
                        pe.wait_ge(squared, c)
                    lo = 2 * (p % 2)
                    if n < GROUP:
                        h = GROUP * g + n
                        q, k = Qs[:, h % HALF, h // HALF, :], Ks[:, h % HALF, h // HALF, :]
                        for j in (0, 1, 3):
                            at = TILE_AT[j]
                            ins = pe.matmul(psum[:, lo + at // BANK, at % BANK:at % BANK + L - j * P],
                                            k[:, j * P:(j + 1) * P], q[:, j * P:L], start=True, stop=True)
                    else:
                        for a in range(GROUP):
                            h = GROUP * g + a
                            q, k = Qs[:, h % HALF, h // HALF, :], Ks[:, h % HALF, h // HALF, :]
                            at = a * 256
                            ins = pe.matmul(psum[:, lo + at // BANK, at % BANK:at % BANK + 256],
                                            k[:, 2 * P:3 * P], q[:, 2 * P:L], start=True, stop=True)
                    ins.then_inc(scores_ready, 1)

            def values(b, g, left):
                if absent(b):
                    return
                pe.wait_ge(masked, count(masked, b, 3 * g + 3))
                if g == 0:
                    pe.wait_ge(v_ready, count(v_ready, b, 2))
                if left:
                    pe.wait_ge(left[0], left[1])
                for j in range(T):
                    for a in range(GROUP):
                        at = a * 1024 + TILE_AT[j] if j != 2 else TILE2_AT + a * 256
                        ins = pe.matmul(psum[32 * a:32 * a + 32, SUM_BANK[g], j * P:L], V1[:, j, GROUP * g + a, :],
                                        A[:, g % 2, at:at + L - j * P], start=(j == 0), stop=(j == T - 1))
                ins.then_inc(values_summed, 1)

            def o_rows(b, t, left):
                if absent(b):
                    return
                if t == 0:
                    pe.wait_ge(oT_ready, count(oT_ready, b, GROUPS))
                if left:
                    pe.wait_ge(left[0], left[1])
                for g in range(GROUPS):
                    ins = pe.transpose(psum[:, O_BANK[t], g * P:(g + 1) * P], oT[:, g, t * P:(t + 1) * P], ident[:, :])
                ins.then_inc(o_in_psum, 1)

            def onT_transpose(b, k, left):
                if absent(b):
                    return
                if k == 0:
                    pe.wait_ge(o_normed, count(o_normed, b, T))
                if left:
                    pe.wait_ge(left[0], left[1])
                transpose_rows(psum[:, ONT_BANK[k], :], tok, k).then_inc(onT_in_psum, 1)

            def wo_product(b, j, left):
                if absent(b):
                    return
                if j == 0:
                    pe.wait_ge(onT_ready, count(onT_ready, b, KD))
                if left:
                    pe.wait_ge(left[0], left[1])
                token_product(psum[:, WO_BANK[j], :], j, onT, wo, KD).then_inc(wo_in_psum, 1)

            def norm2_transpose(b, k, left):
                if absent(b):
                    return
                if k == 0:
                    pe.wait_ge(xn2_ready, count(xn2_ready, b, 1))
                if left:
                    pe.wait_ge(left[0], left[1])
                transpose_rows(psum[:, XN2T_BANK[k], :], xn2, k).then_inc(xn2T_in_psum, 1)

            def context_up(b, f, left):
                if absent(b):
                    return
                if f == 0:
                    pe.wait_ge(ctx_loaded, count(ctx_loaded, b, 32))
                    pe.wait_ge(xn2T_ready, count(xn2T_ready, b, KD))
                if left:
                    pe.wait_ge(left[0], left[1])
                product(psum[:, UPCTX_BANK[f], :], [(ctxT[:, k, f * P:(f + 1) * P], xn2T[:, k, :]) for k in range(KD)])\
                    .then_inc(h1_in_psum, 1)

            def context_down(b, j, left):
                if absent(b):
                    return
                if j == 0:
                    pe.wait_ge(gated, count(gated, b, T))
                if left:
                    pe.wait_ge(left[0], left[1])
                token_product(psum[:, DOWNCTX_BANK[j], :], j, gT, ctxR, T).then_inc(mix_in_psum, 1)

            def xqT_transpose(b, left):
                if absent(b):
                    return
                pe.wait_ge(xq_ready, count(xq_ready, b, 1))
                if left:
                    pe.wait_ge(left[0], left[1])
                wide = psum[:, XQT_BANK, :].bitcast(bf16)
                for k in range(KD):
                    for t in range(T):
                        ins = pe.transpose(wide[:, k * L + t * P:k * L + (t + 1) * P],
                                           xq[:, t, k * P:(k + 1) * P], identb[:, :])
                ins.then_inc(xqT_in_psum, 1)

            def spread_scales(bank, s):
                for t in range(T):
                    ins = pe.transpose(bank[:, t * P:(t + 1) * P], s[:, t:t + 1].to_broadcast([P, P]), ident[:, :])
                return ins

            def spread_token_scales(b, left):
                if absent(b):
                    return
                pe.wait_ge(quantise_chain, count(quantise_chain, b, 5))
                if left:
                    pe.wait_ge(left[0], left[1])
                spread_scales(psum[:, SCALE_BANK, :], sdq).then_inc(s_in_psum, 1)

            def ffn_up(b, f, left):
                if absent(b):
                    return
                if f == 0:
                    pe.wait_ge(xqT_ready, count(xqT_ready, b, 1))
                if left:
                    pe.wait_ge(left[0], left[1])
                product(psum[:, UP_BANK[f], :], [(w_up_q[:, k, f * P:(f + 1) * P], xqT[:, k, :]) for k in range(KD)])\
                    .then_inc(up_in_psum, 1)

            def hidden_max_rows(b, left):
                if absent(b):
                    return
                pe.wait_ge(am_ready, count(am_ready, b, 2))
                if left:
                    pe.wait_ge(left[0], left[1])
                for t in range(T):
                    ins = pe.transpose(psum[:, MAX_BANK, t * P:(t + 1) * P], am[:, t * P:(t + 1) * P], ident[:, :])
                ins.then_inc(amT_in_psum, 1)

            def spread_hidden_scales(b, left):
                if absent(b):
                    return
                pe.wait_ge(s2_ready, count(s2_ready, b, 1))
                if left:
                    pe.wait_ge(left[0], left[1])
                spread_scales(psum[:, HSCALE_BANK, :], sc4).then_inc(s2_in_psum, 1)

            def ffn_down(b, j, left):
                if absent(b):
                    return
                if j == 0:
                    pe.wait_ge(hq_ready, count(hq_ready, b, NF // 2))
                if left:
                    pe.wait_ge(left[0], left[1])
                token_product(psum[:, DOWN_BANK[j], :], j, hq, w_dn_q, NF).then_inc(down_in_psum, 1)

            def weights_total():
                pe.wait_ge(w_rest_loaded, 16 * 3)
                pe.wait_ge(wsum_ready, 1)
                pe.matmul(psum[:, 0, 0:2], ones[:, :], wsum[:, :], start=True, stop=True).then_inc(wtotal_ready, 1)
                pe.wait_ge(setup_dve, 1)

            def keep_warm(products):
                for _ in range(products):
                    pe.matmul(psum[:, 0, 0:P], ones[:, :], ones[:, :], start=True, stop=True)

            def iteration(i, weights=False, last=False):
                if last and i == (B - 1) + 2:
                    keep_warm(14)
                norm2_transpose(i - 2, 0, latest((v_ready, i - 1, 2), (x1_ready, i - 2, 1)))
                norm2_transpose(i - 2, 1, latest((hs_ready, i - 3, 5), (v_ready, i - 1, 1)))
                scores(i - 1, 7)
                values(i - 1, 0, latest((hs_ready, i - 3, 6), (x1_ready, i - 2, 2), (rest_ready, i - 1, 2)))
                ffn_up(i - 3, 7, latest((xn2T_ready, i - 2, 2), (hs_ready, i - 3, 5)))
                context_up(i - 2, 0, latest((xn2T_ready, i - 2, 1)))
                scores(i - 1, 8, 9)
                context_up(i - 2, 1, latest((hs_ready, i - 3, 7), (o_normed, i - 2, 3)))
                scores(i - 1, 10)
                norm1_transpose(i, 0, latest((hs_ready, i - 3, 8), (xn2T_ready, i - 2, 2), (v_ready, i - 1, 1)))
                scores(i - 1, 11)
                norm1_transpose(i, 1, latest((oT_ready, i - 1, 1)))
                values(i - 1, 1, latest((xn1T_ready, i, 1), (hs_ready, i - 3, 8)))
                context_up(i - 2, 2, latest((xn1T_ready, i, 2), (oT_ready, i - 1, 1), (hs_ready, i - 3, 6)))
                scores(i - 1, 12, 13)
                qk(i, 0, latest((oT_ready, i - 1, 2), (xn1T_ready, i, 1)))
                if last and i == (B - 2) + 3:
                    keep_warm(20)
                hidden_max_rows(i - 3, latest((gated, i - 2, 1), (x2_ready, i - 3, 1)))
                context_up(i - 2, 3, latest((gated, i - 2, 2)))
                if last and i == (B - 1) + 3:
                    keep_warm(10)
                spread_hidden_scales(i - 3, latest((hidden_chain, i - 3, 1)))
                scores(i - 1, 14, 15)
                qk(i, 1, latest((gated, i - 2, 3), (xn1T_ready, i, 2)))
                if last and i == (B - 1) + 2:
                    keep_warm(10)
                context_down(i - 2, 0, latest((s2B_ready, i - 3, 1), (gated, i - 2, 1)))
                scores(i - 1, 16)
                if last and i == (B - 1) + 3:
                    keep_warm(28)
                ffn_down(i - 3, 0, latest((rest_ready, i, 1), (oT_ready, i - 1, 2), (hs_ready, i - 3, 8)))
                ffn_down(i - 3, 1, latest((gated, i - 2, 4), (hs_ready, i - 3, 7)))
                context_down(i - 2, 1, latest((out_ready, i - 3, 1), (rest_ready, i, 1)))
                scores(i - 1, 17)
                qk(i, 2, latest((x2_ready, i - 2, 1), (v_ready, i - 1, 2)))
                scores(i - 1, 18, 19)
                qk(i, 3, latest((x2_ready, i - 2, 2), (rest_ready, i, 1)))
                values(i - 1, 2, latest((rest_ready, i, 2), (gated, i - 2, 3)))
                values(i - 1, 3, latest((out_ready, i - 3, 2), (gated, i - 2, 4)))
                if last and i == (B - 1) + 2:
                    keep_warm(30)
                spread_token_scales(i - 2, latest((oT_ready, i - 1, 3), (gated, i - 2, 3)))
                xqT_transpose(i - 2, latest((rest_ready, i, 4), (x2_ready, i - 2, 2)))
                o_rows(i - 1, 0, latest((rest_ready, i, 3), (x2_ready, i - 2, 1)))
                o_rows(i - 1, 1, latest((sB_ready, i - 2, 1), (oT_ready, i - 1, 3)))
                o_rows(i - 1, 2, latest((oT_ready, i - 1, 4)))
                ffn_up(i - 2, 0, latest((xqT_ready, i - 2, 1)))
                o_rows(i - 1, 3, latest((o_normed, i - 1, 1)))
                ffn_up(i - 2, 1, latest((o_normed, i - 1, 2), (sB_ready, i - 2, 1)))
                v(i, 0, latest((hs_ready, i - 2, 1), (rest_ready, i, 4)))
                onT_transpose(i - 1, 0, latest((o_normed, i - 1, 4)))
                onT_transpose(i - 1, 1, latest((hs_ready, i - 2, 2), (o_normed, i - 1, 2)))
                ffn_up(i - 2, 2, latest((v_ready, i, 1), (hs_ready, i - 2, 1)))
                ffn_up(i - 2, 3, latest((o_normed, i - 1, 3), (out_ready, i - 3, 2)))
                wo_product(i - 1, 0, latest((onT_ready, i - 1, 1)))
                ffn_up(i - 2, 4, latest((hs_ready, i - 2, 3)))
                if weights:
                    weights_total()
                scores(i, 0, 1)
                wo_product(i - 1, 1, latest((onT_ready, i - 1, 2)))
                scores(i, 2, 3)
                v(i, 1, latest((x1_ready, i - 1, 1), (rest_ready, i, 3)))
                scores(i, 4, 5)
                ffn_up(i - 2, 5, latest((x1_ready, i - 1, 2), (hs_ready, i - 2, 2)))
                ffn_up(i - 2, 6, latest((hs_ready, i - 2, 4)))
                scores(i, 6)

            pe.wait_ge(consts_ready, 2)
            keep_warm(20)
            pe.wait_ge(consts_ready, 9)
            pe.wait_ge(w_qkv_loaded, 16 * 2)
            for i in range(LEAD):
                if i == 2:
                    pe.wait_ge(weights_quantised, 2)
                iteration(i, weights=(i == 0))
            with pe.Fori(LEAD, B) as i:
                iteration(i)
            for i in range(B, B + DEPTH):
                iteration(i, last=True)


def kernel(**inputs):
    import numpy as np
    import concourse.bacc as bacc
    from concourse.bass_utils import run_bass_kernel_spmd

    a = {n: np.asarray(v) for n, v in inputs.items()}
    D = a["x"].shape[2]
    H = 16
    P = 128

    def dims_outside_heads(w):
        return w.reshape(D, 2, H // 2, D // H).transpose(0, 1, 3, 2).reshape(D, D)

    conv_w = a["L0_ffn_conv_w"]
    arrays = {
        "x": a["x"],
        "ctx_rows": a["ctx_1024"],
        "ctx_cols": a["ctx_1024"].transpose(0, 2, 1),
        "w_qk": np.concatenate([dims_outside_heads(a["L0_attn_Wq"]), dims_outside_heads(a["L0_attn_Wk"])], axis=1),
        "w_v": a["L0_attn_Wv"],
        "w_o": a["L0_attn_Wo"],
        "w_up": a["L0_ffn_w1"].T,
        "conv_w": conv_w.reshape(-1, P, 3).transpose(1, 0, 2),
        "conv_b": a["L0_ffn_conv_b"].reshape(-1, P).T,
        "w_down": a["L0_ffn_w2"].T,
    }
    arrays = {n: np.ascontiguousarray(v) for n, v in arrays.items()}
    nc = bacc.Bacc("TRN2", target_bir_lowering=False, num_devices=1, dynamic_dma_scratch_size=1024)
    args = [nc.dram_tensor(n, v.shape, mybir.dt.from_np(v.dtype), kind="ExternalInput").ap()
            for n, v in arrays.items()]
    out = nc.dram_tensor("out", a["x"].shape, mybir.dt.from_np(a["x"].dtype), kind="ExternalOutput").ap()
    decoder_layer(nc, *args, out)
    return run_bass_kernel_spmd(nc, [arrays], core_ids=[0]).results[0]["out"]
```
